# Optimizing a Trainium2 kernel written in Bass

```python
import numpy as np
import jax
import jax.numpy as jnp

def _softmax(x, axis=-1):
    return jax.nn.softmax(x, axis=axis)

def _gelu(x):
    return jax.nn.gelu(x, approximate=True)

def _silu(x):
    return jax.nn.silu(x)

def _sigmoid(x):
    return jax.nn.sigmoid(x)

def _layernorm(x, axis=-1, eps=1e-05):
    m = jnp.mean(x, axis=axis, keepdims=True)
    v = jnp.var(x, axis=axis, keepdims=True)
    return (x - m) / jnp.sqrt(v + eps)

def _scatter_add(tgt, idx, src, axis=0):
    return tgt.at[idx].add(src)

def _segment_sum(src, seg, n):
    return jax.ops.segment_sum(src, seg, n)
kernel_name = 'mk_perceiver_d1_seqx_r2_47e76e'

def setup_inputs(seed: int=0):
    np.random.seed(seed)
    _w = jnp.asarray

    def _rec_inputs():
        import jax
        import jax.numpy as jnp
        _rk = jax.random.key(seed)
        x = -0.0002928 + 1 * jax.random.normal(jax.random.fold_in(_rk, 1), (8, 64, 512), jnp.float32)
        _lenS = 64 - jax.random.randint(jax.random.fold_in(_rk, 7), (8,), 0, max(1, 64 // 4) + 1, jnp.int32)
        _lenS2 = 1601 - jax.random.randint(jax.random.fold_in(_rk, 8), (8,), 0, max(1, 1601 // 4) + 1, jnp.int32)
        _ctx_1024P = jax.random.normal(jax.random.fold_in(_rk, 11), (8, 16, 512), jnp.float32)
        _ctx_1024c = jax.random.dirichlet(jax.random.fold_in(_rk, 511), 0.3 * jnp.ones((16,), jnp.float32), (8, 1601))
        _ctx_1024t = jnp.einsum('bsk,bkd->bsd', _ctx_1024c, _ctx_1024P)
        _ctx_1024t = _ctx_1024t * jax.lax.rsqrt(jnp.mean(jnp.square(_ctx_1024t)) + 1e-12) * 0.953939
        ctx_1024 = -1.39393e-06 + 0.999914 * (_ctx_1024t + 0.3 * jax.random.normal(jax.random.fold_in(_rk, 611), (8, 1601, 512), jnp.float32))
        return (x, ctx_1024)
    x, ctx_1024 = _rec_inputs()

    def _L0_xattn_setup():
        import jax, jax.numpy as jnp
        import numpy as np
        D_MODEL = 512
        N_HEADS = 16
        D_K = D_MODEL // N_HEADS
        key = jax.random.key(seed)
        ks = jax.random.split(key, 11)
        B, L, S = (2, 1024, 1024)
        scale = 1.0 / np.sqrt(D_MODEL)
        return {'x_q': jax.random.normal(ks[0], (B, L, D_MODEL), jnp.float32), 'x_k': jax.random.normal(ks[1], (B, S, D_MODEL), jnp.float32), 'x_v': jax.random.normal(ks[2], (B, S, D_MODEL), jnp.float32), 'W_Q': jax.random.normal(ks[3], (D_MODEL, D_MODEL), jnp.float32) * scale, 'b_Q': jax.random.normal(ks[4], (D_MODEL,), jnp.float32) * 0.01, 'W_K': jax.random.normal(ks[5], (D_MODEL, D_MODEL), jnp.float32) * scale, 'b_K': jax.random.normal(ks[6], (D_MODEL,), jnp.float32) * 0.01, 'W_V': jax.random.normal(ks[7], (D_MODEL, D_MODEL), jnp.float32) * scale, 'b_V': jax.random.normal(ks[8], (D_MODEL,), jnp.float32) * 0.01, 'W_O': jax.random.normal(ks[9], (D_MODEL, D_MODEL), jnp.float32) * scale, 'b_O': jax.random.normal(ks[10], (D_MODEL,), jnp.float32) * 0.01}
    _L0_xattn_all = _L0_xattn_setup()
    _L0_xattn_in = {k: v for k, v in _L0_xattn_all.items() if k in ('W_Q', 'b_Q', 'W_K', 'b_K', 'W_V', 'b_V', 'W_O', 'b_O')}
    del _L0_xattn_all

    def _L0_attn_setup():
        import jax, jax.numpy as jnp
        import numpy as np
        B, N, DM, H, FF = (8, 1024, 512, 16, 2048)
        D = DM // H // 2
        LAMBDA_INIT = 0.8 - 0.6 * float(np.exp(-0.3 * 1.0))

        def _layernorm(x, g, b, eps=1e-05):
            mu = jnp.mean(x, axis=-1, keepdims=True)
            var = jnp.mean(jnp.square(x - mu), axis=-1, keepdims=True)
            return (x - mu) * jax.lax.rsqrt(var + eps) * g + b

        def _rmsnorm(x, eps=1e-05):
            return x * jax.lax.rsqrt(jnp.mean(x * x, axis=-1, keepdims=True) + eps)

        def _diff_attn(x, Wq, Wk, Wv, lq1, lq2, lk1, lk2, Wo, bo):
            b, n, d = x.shape
            scale = D ** (-0.5)
            q = (x @ Wq.T).reshape(b, n, H, D, 2).transpose(0, 1, 4, 2, 3).reshape(b, n, 2 * H, D) * scale
            k = (x @ Wk.T).reshape(b, n, H, D, 2).transpose(0, 1, 4, 2, 3).reshape(b, n, 2 * H, D)
            v = (x @ Wv.T).reshape(b, n, H, 2 * D).transpose(0, 2, 1, 3)
            att = jnp.einsum('bnqd,bnkd->bnqk', q, k)
            att = jnp.nan_to_num(att)
            att = jax.nn.softmax(att.astype(jnp.float32), axis=-1)
            lam = jnp.exp(jnp.sum(lq1 * lk1)) - jnp.exp(jnp.sum(lq2 * lk2)) + LAMBDA_INIT
            att6 = att.reshape(b, n, 2, H, 2, H)
            att2 = att6[:, :, 0, :, 0, :] - lam * att6[:, :, 1, :, 1, :]
            out = jnp.einsum('bnah,bhnd->bnad', att2, v)
            out = _rmsnorm(out) * (1.0 - LAMBDA_INIT)
            out = out.reshape(b, n, d)
            return out @ Wo.T + bo
        key = jax.random.key(seed)
        ks = jax.random.split(key, 12)
        p = lambda k, sh, s=0.02: jax.random.normal(k, sh, jnp.float32) * s
        return {'x': jax.random.normal(ks[0], (B, N, DM), jnp.float32), 'Wq': p(ks[1], (DM, DM)), 'Wk': p(ks[2], (DM, DM)), 'Wv': p(ks[3], (DM, DM)), 'lq1': p(ks[4], (D,), 0.1), 'lq2': p(ks[5], (D,), 0.1), 'lk1': p(ks[6], (D,), 0.1), 'lk2': p(ks[7], (D,), 0.1), 'Wo': p(ks[8], (DM, DM)), 'bo': jnp.zeros((DM,), jnp.float32), 'ln1_g': jnp.ones((DM,), jnp.float32), 'ln1_b': jnp.zeros((DM,), jnp.float32), 'ln2_g': jnp.ones((DM,), jnp.float32), 'ln2_b': jnp.zeros((DM,), jnp.float32), 'W1': p(ks[9], (FF, DM)), 'b1': jnp.zeros((FF,), jnp.float32), 'W2': p(ks[10], (DM, FF)), 'b2': jnp.zeros((DM,), jnp.float32)}
    _L0_attn_all = _L0_attn_setup()
    _L0_attn_in = {k: v for k, v in _L0_attn_all.items() if k in ('Wq', 'Wk', 'Wv', 'lq1', 'lq2', 'lk1', 'lk2', 'Wo', 'bo', 'ln1_g', 'ln1_b', 'ln2_g', 'ln2_b', 'W1', 'b1', 'W2', 'b2')}
    del _L0_attn_all

    def _L0_ffn_setup():
        import jax, jax.numpy as jnp
        import numpy as np
        H = 512
        I = 256
        E = 32
        TOP_K = 6
        N_GROUP = 8
        TOPK_GROUP = 4
        SCALE = 2.5
        N_SHARED = 2
        SI = I * N_SHARED
        B, S = (2, 512)
        key = jax.random.key(seed)
        ks = jax.random.split(key, 8)
        x = jax.random.normal(ks[0], (B, S, H), jnp.float32)
        gate_weight = jax.random.normal(ks[1], (E, H), jnp.float32) * 0.02
        e_score_correction_bias = jax.random.normal(ks[2], (E,), jnp.float32) * 0.01
        experts_gate_up = jax.random.normal(ks[3], (E, 2 * I, H), jnp.float32) * 0.02
        experts_down = jax.random.normal(ks[4], (E, H, I), jnp.float32) * 0.02
        shared_gate_w = jax.random.normal(ks[5], (SI, H), jnp.float32) * 0.02
        shared_up_w = jax.random.normal(ks[6], (SI, H), jnp.float32) * 0.02
        shared_down_w = jax.random.normal(ks[7], (H, SI), jnp.float32) * 0.02
        return {'x': x, 'gate_weight': gate_weight, 'e_score_correction_bias': e_score_correction_bias, 'experts_gate_up': experts_gate_up, 'experts_down': experts_down, 'shared_gate_w': shared_gate_w, 'shared_up_w': shared_up_w, 'shared_down_w': shared_down_w}
    _L0_ffn_all = _L0_ffn_setup()
    _L0_ffn_in = {k: v for k, v in _L0_ffn_all.items() if k in ('gate_weight', 'e_score_correction_bias', 'experts_gate_up', 'experts_down', 'shared_gate_w', 'shared_up_w', 'shared_down_w')}
    del _L0_ffn_all
    return {'x': x, 'ctx_1024': ctx_1024, 'L0_xattn_W_Q': _L0_xattn_in['W_Q'], 'L0_xattn_b_Q': _L0_xattn_in['b_Q'], 'L0_xattn_W_K': _L0_xattn_in['W_K'], 'L0_xattn_b_K': _L0_xattn_in['b_K'], 'L0_xattn_W_V': _L0_xattn_in['W_V'], 'L0_xattn_b_V': _L0_xattn_in['b_V'], 'L0_xattn_W_O': _L0_xattn_in['W_O'], 'L0_xattn_b_O': _L0_xattn_in['b_O'], 'L0_attn_Wq': _L0_attn_in['Wq'], 'L0_attn_Wk': _L0_attn_in['Wk'], 'L0_attn_Wv': _L0_attn_in['Wv'], 'L0_attn_lq1': _L0_attn_in['lq1'], 'L0_attn_lq2': _L0_attn_in['lq2'], 'L0_attn_lk1': _L0_attn_in['lk1'], 'L0_attn_lk2': _L0_attn_in['lk2'], 'L0_attn_Wo': _L0_attn_in['Wo'], 'L0_attn_bo': _L0_attn_in['bo'], 'L0_attn_ln1_g': _L0_attn_in['ln1_g'], 'L0_attn_ln1_b': _L0_attn_in['ln1_b'], 'L0_attn_ln2_g': _L0_attn_in['ln2_g'], 'L0_attn_ln2_b': _L0_attn_in['ln2_b'], 'L0_attn_W1': _L0_attn_in['W1'], 'L0_attn_b1': _L0_attn_in['b1'], 'L0_attn_W2': _L0_attn_in['W2'], 'L0_attn_b2': _L0_attn_in['b2'], 'L0_ffn_gate_weight': _L0_ffn_in['gate_weight'], 'L0_ffn_e_score_correction_bias': _L0_ffn_in['e_score_correction_bias'], 'L0_ffn_experts_gate_up': _L0_ffn_in['experts_gate_up'], 'L0_ffn_experts_down': _L0_ffn_in['experts_down'], 'L0_ffn_shared_gate_w': _L0_ffn_in['shared_gate_w'], 'L0_ffn_shared_up_w': _L0_ffn_in['shared_up_w'], 'L0_ffn_shared_down_w': _L0_ffn_in['shared_down_w']}

def reference(x, ctx_1024, L0_xattn_W_Q, L0_xattn_b_Q, L0_xattn_W_K, L0_xattn_b_K, L0_xattn_W_V, L0_xattn_b_V, L0_xattn_W_O, L0_xattn_b_O, L0_attn_Wq, L0_attn_Wk, L0_attn_Wv, L0_attn_lq1, L0_attn_lq2, L0_attn_lk1, L0_attn_lk2, L0_attn_Wo, L0_attn_bo, L0_attn_ln1_g, L0_attn_ln1_b, L0_attn_ln2_g, L0_attn_ln2_b, L0_attn_W1, L0_attn_b1, L0_attn_W2, L0_attn_b2, L0_ffn_gate_weight, L0_ffn_e_score_correction_bias, L0_ffn_experts_gate_up, L0_ffn_experts_down, L0_ffn_shared_gate_w, L0_ffn_shared_up_w, L0_ffn_shared_down_w):
    import jax
    import jax.numpy as jnp

    def _L0_xattn_ref(x_q, x_k, x_v, W_Q, b_Q, W_K, b_K, W_V, b_V, W_O, b_O):
        import jax, jax.numpy as jnp
        import numpy as np
        D_MODEL = 512
        N_HEADS = 16
        D_K = D_MODEL // N_HEADS
        B, L, _ = x_q.shape
        S = x_k.shape[1]
        H, dk = (N_HEADS, D_K)
        Q = (x_q @ W_Q + b_Q).reshape(B, L, H, dk).transpose(0, 2, 1, 3)
        K = (x_k @ W_K + b_K).reshape(B, S, H, dk).transpose(0, 2, 1, 3)
        V = (x_v @ W_V + b_V).reshape(B, S, H, dk).transpose(0, 2, 1, 3)
        scores = jnp.einsum('bhld,bhsd->bhls', Q, K) / jnp.sqrt(jnp.float32(dk))
        attn = jax.nn.softmax(scores, axis=-1)
        ctx = jnp.einsum('bhls,bhsd->bhld', attn, V)
        ctx = ctx.transpose(0, 2, 1, 3).reshape(B, L, H * dk)
        out = ctx @ W_O + b_O
        return out

    def _L0_attn_ref(x, Wq, Wk, Wv, lq1, lq2, lk1, lk2, Wo, bo, ln1_g, ln1_b, ln2_g, ln2_b, W1, b1, W2, b2):
        import jax, jax.numpy as jnp
        import numpy as np
        B, N, DM, H, FF = (8, 1024, 512, 16, 2048)
        D = DM // H // 2
        LAMBDA_INIT = 0.8 - 0.6 * float(np.exp(-0.3 * 1.0))

        def _layernorm(x, g, b, eps=1e-05):
            mu = jnp.mean(x, axis=-1, keepdims=True)
            var = jnp.mean(jnp.square(x - mu), axis=-1, keepdims=True)
            return (x - mu) * jax.lax.rsqrt(var + eps) * g + b

        def _rmsnorm(x, eps=1e-05):
            return x * jax.lax.rsqrt(jnp.mean(x * x, axis=-1, keepdims=True) + eps)

        def _diff_attn(x, Wq, Wk, Wv, lq1, lq2, lk1, lk2, Wo, bo):
            b, n, d = x.shape
            scale = D ** (-0.5)
            q = (x @ Wq.T).reshape(b, n, H, D, 2).transpose(0, 1, 4, 2, 3).reshape(b, n, 2 * H, D) * scale
            k = (x @ Wk.T).reshape(b, n, H, D, 2).transpose(0, 1, 4, 2, 3).reshape(b, n, 2 * H, D)
            v = (x @ Wv.T).reshape(b, n, H, 2 * D).transpose(0, 2, 1, 3)
            att = jnp.einsum('bnqd,bnkd->bnqk', q, k)
            att = jnp.nan_to_num(att)
            att = jax.nn.softmax(att.astype(jnp.float32), axis=-1)
            lam = jnp.exp(jnp.sum(lq1 * lk1)) - jnp.exp(jnp.sum(lq2 * lk2)) + LAMBDA_INIT
            att6 = att.reshape(b, n, 2, H, 2, H)
            att2 = att6[:, :, 0, :, 0, :] - lam * att6[:, :, 1, :, 1, :]
            out = jnp.einsum('bnah,bhnd->bnad', att2, v)
            out = _rmsnorm(out) * (1.0 - LAMBDA_INIT)
            out = out.reshape(b, n, d)
            return out @ Wo.T + bo
        skip = x
        h = _layernorm(x, ln1_g, ln1_b)
        src2 = _diff_attn(h, Wq, Wk, Wv, lq1, lq2, lk1, lk2, Wo, bo)
        conn = skip + src2
        skip2 = conn
        h2 = _layernorm(conn, ln2_g, ln2_b)
        src3 = jax.nn.relu(h2 @ W1.T + b1) @ W2.T + b2
        return skip2 + src3

    def _L0_ffn_ref(x, gate_weight, e_score_correction_bias, experts_gate_up, experts_down, shared_gate_w, shared_up_w, shared_down_w):
        import jax, jax.numpy as jnp
        import numpy as np
        H = 512
        I = 256
        E = 32
        TOP_K = 6
        N_GROUP = 8
        TOPK_GROUP = 4
        SCALE = 2.5
        N_SHARED = 2
        SI = I * N_SHARED
        B, S = (2, 512)
        b, s, h = x.shape
        xf = x.reshape(-1, h)
        T = xf.shape[0]
        logits = xf.astype(jnp.float32) @ gate_weight.astype(jnp.float32).T
        scores = jax.nn.sigmoid(logits)
        sfc = scores + e_score_correction_bias[None, :]
        gs = E // N_GROUP
        group_scores = sfc.reshape(T, N_GROUP, gs).max(axis=-1)
        _, gidx = jax.lax.top_k(group_scores, TOPK_GROUP)
        gmask = jnp.zeros((T, N_GROUP), bool).at[jnp.arange(T)[:, None], gidx].set(True)
        smask = jnp.repeat(gmask, gs, axis=1)
        masked = jnp.where(smask, sfc, 0.0)
        _, topk_idx = jax.lax.top_k(masked, TOP_K)
        tw = jnp.take_along_axis(scores, topk_idx, axis=1)
        tw = tw / (tw.sum(-1, keepdims=True) + 1e-20)
        tw = (tw * SCALE).astype(xf.dtype)
        combine = jnp.zeros((T, E), xf.dtype).at[jnp.arange(T)[:, None], topk_idx].add(tw)

        def expert_step(acc, inp):
            gu, dn, c = inp
            g = xf @ gu[:I].T
            u = xf @ gu[I:].T
            o = jax.nn.silu(g) * u @ dn.T
            return (acc + c[:, None] * o, None)
        routed, _ = jax.lax.scan(expert_step, jnp.zeros_like(xf), (experts_gate_up, experts_down, combine.T))
        sh = jax.nn.silu(xf @ shared_gate_w.T) * (xf @ shared_up_w.T)
        shared_out = sh @ shared_down_w.T
        return (routed + shared_out).reshape(b, s, h)
    x = x + _L0_xattn_ref(_layernorm(x, axis=-1), ctx_1024, ctx_1024, L0_xattn_W_Q, L0_xattn_b_Q, L0_xattn_W_K, L0_xattn_b_K, L0_xattn_W_V, L0_xattn_b_V, L0_xattn_W_O, L0_xattn_b_O)
    x = x + _L0_attn_ref(_layernorm(x, axis=-1), L0_attn_Wq, L0_attn_Wk, L0_attn_Wv, L0_attn_lq1, L0_attn_lq2, L0_attn_lk1, L0_attn_lk2, L0_attn_Wo, L0_attn_bo, L0_attn_ln1_g, L0_attn_ln1_b, L0_attn_ln2_g, L0_attn_ln2_b, L0_attn_W1, L0_attn_b1, L0_attn_W2, L0_attn_b2)
    x = x + _L0_ffn_ref(_layernorm(x, axis=-1), L0_ffn_gate_weight, L0_ffn_e_score_correction_bias, L0_ffn_experts_gate_up, L0_ffn_experts_down, L0_ffn_shared_gate_w, L0_ffn_shared_up_w, L0_ffn_shared_down_w)
    return x

_drawn_inputs = setup_inputs


def setup_inputs(seed=0):
    import zlib

    import numpy as np

    out = dict(_drawn_inputs(seed))
    spreads = {'L0_attn_bo': (0.0, 0.1),
     'L0_attn_ln1_g': (1.0, 0.2),
     'L0_attn_ln1_b': (0.0, 0.478),
     'L0_attn_ln2_g': (1.0, 0.6),
     'L0_attn_ln2_b': (0.0, 0.587),
     'L0_attn_b1': (0.0, 0.277),
     'L0_attn_b2': (0.0, 0.1)}
    factors = {'L0_xattn_b_Q': 8.0,
     'L0_xattn_b_K': 64.0,
     'L0_xattn_b_V': 6.593,
     'L0_xattn_b_O': 6.174,
     'L0_attn_lq1': 8.0,
     'L0_attn_lq2': 8.0,
     'L0_attn_lk1': 7.121,
     'L0_attn_lk2': 8.0,
     'L0_ffn_gate_weight': 3.832,
     'L0_ffn_e_score_correction_bias': 8.0,
     'L0_ffn_experts_gate_up': 3.447,
     'L0_ffn_experts_down': 3.441,
     'L0_ffn_shared_gate_w': 3.318,
     'L0_ffn_shared_up_w': 3.255,
     'L0_ffn_shared_down_w': 3.239}
    for name, (base, spread) in spreads.items():
        noise = np.random.default_rng([zlib.crc32(name.encode()), seed]).standard_normal(out[name].shape)
        drawn = base * np.exp(spread * noise) if base else spread * noise
        out[name] = jnp.asarray(drawn.astype(out[name].dtype))
    for name, factor in factors.items():
        out[name] = (out[name] * factor).astype(out[name].dtype)
    return out
```

```python
from contextlib import ExitStack

import numpy as np

import concourse.bass as bass
from concourse import mybir

F32 = mybir.dt.float32
F32R = mybir.dt.float32r
ALU = mybir.AluOpType
ACT = mybir.ActivationFunctionType
AX = mybir.AxisListType

P = 128
B, L, D = 8, 64, 512
S = 1601
T = B * L
TT = T // P
KD = D // P
EPS = 1e-5

NH, DK = 16, 32
NCH = 4
CW = 402
SP_ = NCH * CW
ST = -(-S // P)
LAST = S - (ST - 1) * P
NV = -(-ST // 2)
SC_CHUNKS = [(0, 512, 512), (512, 512, 512), (1024, 512, 512), (1536, 66, 65)]
V_BANK = [6, 7, 4, 5, 6, 7, 5]

H2, D2 = 16, 16
FF = 2048
LAMBDA_INIT = 0.8 - 0.6 * float(np.exp(-0.3 * 1.0))
FMAX = float(np.finfo(np.float32).max)

E, I = 32, 256
NG, GS = 8, 4
TOPK, TOPKG = 6, 4
SCALE = 2.5
NX = E + 2


def f32(ap):
    return ap.bitcast(F32)


def mm3(nc, out, a_hi, a_lo, b_hi, b_lo, start, stop):
    nc.tensor.matmul(out, a_hi, b_hi, start=start, stop=False)
    nc.tensor.matmul(out, a_hi, b_lo, start=False, stop=False)
    return nc.tensor.matmul(out, a_lo, b_hi, start=False, stop=stop)


def queries(nc, a, keep):
    ident, wkv_hi, wkv_lo = keep["ident"], keep["wkv_hi"], keep["wkv_lo"]
    with ExitStack() as ctx:
        def sb(name, shape, dt=F32):
            return ctx.enter_context(nc.sbuf_tensor(name, shape, dt))

        def sem(name):
            return ctx.enter_context(nc.semaphore(name))

        x_sb = sb("x_sb", [P, TT, D])
        stats = sb("stats", [P, TT, 6])
        mv = sb("mv", [P, TT, 2])
        veps = sb("veps", [P, TT])
        std = sb("std", [P, TT])
        rstd = sb("rstd", [P, TT])
        xn = sb("xn", [P, TT, D])
        xnT_hi = sb("xnT_hi", [P, KD, T], F32R)
        xnT_lo = sb("xnT_lo", [P, KD, T], F32R)
        wraw = sb("wraw", [P, 3, KD, D])
        wq_hi = sb("wq_hi", [P, KD, D], F32R)
        wq_lo = sb("wq_lo", [P, KD, D], F32R)
        bq = sb("bq", [P, KD])
        bqs = sb("bqs", [P, KD])
        qf = sb("qf", [P, KD, T])
        qbd = sb("qbd_all", [P, B, 2, 2, 2, P], F32R)
        ps = ctx.enter_context(nc.psum_tensor("ps_q", [P, 8, 512], F32))

        x_loaded = sem("q_x_loaded")
        w_loaded = [sem(f"q_w_loaded{i}") for i in range(3)]
        c_loaded = sem("q_c_loaded")
        bq_loaded = sem("q_bq_loaded")
        dve_step = sem("q_dve_step")
        std_done = sem("q_std_done")
        xn_done = sem("q_xn_done")
        tr_full = sem("q_tr_full")
        xT_hi_done = sem("q_xT_hi_done")
        xT_lo_done = sem("q_xT_lo_done")
        w_hi_done = sem("q_w_hi_done")
        w_lo_done = sem("q_w_lo_done")
        bqs_done = sem("q_bqs_done")
        q_full = sem("q_full")
        qf_done = sem("q_qf_done")
        zero_done = sem("q_zero_done")
        q_hi_done = sem("q_hi_done")
        q_lo_done = sem("q_lo_done")
        q_stored = sem("q_stored")

        block = ctx.enter_context(nc.Block())
        scale = float(DK) ** -0.5

        @block.sync
        def _(sp):
            sp.dma_start(x_sb[:], a["x"].rearrange("(t p) d -> p t d", p=P)).then_inc(x_loaded, 16)
            sp.dma_start(ident[:], a["identity"]).then_inc(c_loaded, 16)
            sp.dma_start(bq[:], a["b_Q"]).then_inc(bq_loaded, 16)
            sp.dma_start(keep["bk"][:], a["b_K"]).then_inc(c_loaded, 16)
            sp.dma_start(keep["bv"][:], a["b_V"]).then_inc(c_loaded, 16)
            for i in range(3):
                sp.dma_start(wraw[:, i], a["w_qkv"][i]).then_inc(w_loaded[i], 16)
            sp.wait_ge(q_hi_done, 4 * KD)
            sp.wait_ge(q_lo_done, 4 * KD)
            sp.dma_start(a["qbd_dram"].rearrange("u p n -> p u n"),
                         f32(qbd[:].rearrange("p b h x g n -> p (b h) (x g n)"))).then_inc(q_stored, 16)
            sp.wait_ge(q_stored, 16)
            sp.wait_ge(c_loaded, 48)

        @block.gpsimd
        def _(pool):
            nc.gpsimd.memset(f32(qbd[:].rearrange("p b h x g n -> p (b h x g n)")), 0.0).then_inc(zero_done, 1)
            for i in range(3):
                pool.wait_ge(w_hi_done, i + 1)
                lo, hi = (wq_lo[:], wq_hi[:]) if i == 0 else (wkv_lo[:, :, D * (i - 1):D * i], wkv_hi[:, :, D * (i - 1):D * i])
                nc.gpsimd.tensor_tensor(lo, wraw[:, i], f32(hi), ALU.subtract).then_inc(w_lo_done, 1)
            for G in range(KD):
                h, g = G // 2, G % 2
                for i in range(4):
                    q = slice(32 * i, 32 * i + 32)
                    c = slice(64 * (i % 2), 64 * (i % 2) + 64)
                    pool.wait_ge(q_hi_done, 4 * G + i + 1)
                    pool.wait_ge(*((q_lo_done, 4 * G + i) if G + i else (w_lo_done, 3)))
                    nc.gpsimd.tensor_tensor(qbd[q, :, h, 1, g, c], qf[q, G, :].rearrange("p (b l) -> p b l", b=B),
                                            f32(qbd[q, :, h, 0, g, c]), ALU.subtract).then_inc(q_lo_done, 1)

        @block.scalar
        def _(act):
            act.wait_ge(w_loaded[0], 16)
            nc.scalar.copy(wq_hi[:], wraw[:, 0]).then_inc(w_hi_done, 1)
            act.wait_ge(dve_step, 3)
            nc.scalar.activation(std[:], veps[:], ACT.Sqrt).then_inc(std_done, 1)
            for k in range(KD):
                act.wait_ge(tr_full, k + 1)
                nc.scalar.copy(xnT_hi[:, k], ps[:, k]).then_inc(xT_hi_done, 1)
            act.wait_ge(bqs_done, 1)
            for G in range(KD):
                act.wait_ge(q_full, G + 1)
                nc.scalar.activation(qf[:, G], ps[:, 4 + G], ACT.Identity, bias=bqs[:, G:G + 1],
                                     scale=scale).then_inc(qf_done, 1)
            for i in range(2):
                act.wait_ge(w_loaded[i + 1], 16)
                nc.scalar.copy(wkv_hi[:, :, D * i:D * (i + 1)], wraw[:, i + 1]).then_inc(w_hi_done, 1)

        @block.vector
        def _(dve):
            nc.vector.memset(keep["ones"][:], 1.0)
            dve.wait_ge(bq_loaded, 16)
            nc.vector.tensor_scalar(bqs[:], bq[:], scale, None, ALU.mult).then_inc(bqs_done, 1)
            dve.wait_ge(x_loaded, 16)
            for t in range(TT):
                ins = nc.vector.bn_stats(stats[:, t], x_sb[:, t])
            ins.then_inc(dve_step, 1)
            dve.wait_ge(dve_step, 1)
            for t in range(TT):
                ins = nc.vector.bn_aggr(mv[:, t], stats[:, t])
            ins.then_inc(dve_step, 1)
            dve.wait_ge(dve_step, 2)
            nc.vector.tensor_scalar(veps[:], mv[:, :, 1], EPS, None, ALU.add).then_inc(dve_step, 1)
            dve.wait_ge(std_done, 1)
            nc.vector.reciprocal(rstd[:], std[:]).then_inc(dve_step, 1)
            dve.wait_ge(dve_step, 4)
            for t in range(TT):
                nc.vector.tensor_scalar(xn[:, t], x_sb[:, t], mv[:, t, 0:1], rstd[:, t:t + 1], ALU.subtract,
                                        ALU.mult).then_inc(xn_done, 1)
            for k in range(KD):
                dve.wait_ge(xT_hi_done, k + 1)
                nc.vector.tensor_tensor(xnT_lo[:, k], ps[:, k], f32(xnT_hi[:, k]), ALU.subtract).then_inc(xT_lo_done, 1)
            dve.wait_ge(zero_done, 1)
            for G in range(KD):
                h, g = G // 2, G % 2
                dve.wait_ge(qf_done, G + 1)
                for i in range(4):
                    q = slice(32 * i, 32 * i + 32)
                    c = slice(64 * (i % 2), 64 * (i % 2) + 64)
                    nc.vector.tensor_copy(qbd[q, :, h, 0, g, c],
                                          qf[q, G, :].rearrange("p (b l) -> p b l", b=B)).then_inc(q_hi_done, 1)

        @block.tensor
        def _(pe):
            pe.wait_ge(c_loaded, 48)
            for k in range(KD):
                for t in range(TT):
                    if k == 0:
                        pe.wait_ge(xn_done, t + 1)
                    ins = nc.tensor.transpose(ps[:, k, P * t:P * t + P], xn[:, t, P * k:P * k + P], ident[:])
                ins.then_inc(tr_full, 1)
            pe.wait_ge(w_lo_done, 1)
            for G in range(KD):
                for k in range(KD):
                    if G == 0:
                        pe.wait_ge(xT_lo_done, k + 1)
                    ins = mm3(nc, ps[:, 4 + G], wq_hi[:, k, P * G:P * G + P], wq_lo[:, k, P * G:P * G + P],
                              xnT_hi[:, k], xnT_lo[:, k], k == 0, k == KD - 1)
                ins.then_inc(q_full, 1)


def cross_attention(nc, a, keep):
    ident, ones, wkv_hi, wkv_lo, bk, oT = (keep[n] for n in ("ident", "ones", "wkv_hi", "wkv_lo", "bk", "oT"))
    with ExitStack() as ctx:
        def sb(name, shape, dt=F32):
            return ctx.enter_context(nc.sbuf_tensor(name, shape, dt))

        def sem(name):
            return ctx.enter_context(nc.semaphore(name))

        craw = sb("craw", [P, 2, KD, CW])
        c_hi = sb("c_hi", [P, KD, SP_], F32R)
        c_lo = sb("c_lo", [P, KD, SP_], F32R)
        kT_hi = sb("kT_hi", [P, 2, SP_], F32R)
        kT_lo = sb("kT_lo", [P, 2, SP_], F32R)
        v_hi = sb("v_hi", [P, ST, 256], F32R)
        v_lo = sb("v_lo", [P, ST, 256], F32R)
        qbd = sb("qbd", [P, 2, 2, 2, P], F32R)
        prob = sb("prob", [P, 4, S])
        pT_hi = sb("pT_hi", [P, 2, 512], F32R)
        pT_lo = sb("pT_lo", [P, 2, 512], F32R)
        pmax = sb("pmax", [P, 2, 4])
        nmax = sb("nmax", [P, 4])
        psums = sb("psums", [P, 4, 2])
        rsum = sb("rsum", [P, 2, 2])
        rinv = sb("rinv", [P, 2, 2])
        diag = sb("diag", [P, 2, 2, P])
        rsb = sb("rsb", [P, 2, 256])
        ps = ctx.enter_context(nc.psum_tensor("ps_x", [P, 8, 512], F32))
        sc = ps[:, 0:4, :].rearrange("p a n -> p (a n)")

        c_loaded = [sem(f"x_c_loaded{i}") for i in range(2)]
        qbd_loaded = [sem(f"x_qbd_loaded{i}") for i in range(2)]
        split_hi = sem("x_split_hi")
        split_done = sem("x_split_done")
        k_full, k_hi_done, k_lo_done = sem("x_k_full"), sem("x_k_hi_done"), sem("x_k_lo_done")
        v_full, v_hi_done, v_lo_done = sem("x_v_full"), sem("x_v_hi_done"), sem("x_v_lo_done")
        sc_full = sem("x_sc_full")
        pmax_done, max_done = sem("x_pmax_done"), sem("x_max_done")
        exp_done = sem("x_exp_done")
        sum_step, diag_done = sem("x_sum_step"), sem("x_diag_done")
        pT_full, pT_hi_done, pT_lo_done = sem("x_pT_full"), sem("x_pT_hi_done"), sem("x_pT_lo_done")
        pv_full, rsb_done, o_done = sem("x_pv_full"), sem("x_rsb_done"), sem("x_o_done")

        block = ctx.enter_context(nc.Block())

        def rows(st):
            return P if st < ST - 1 else LAST

        def tiles(t):
            return [st for st in (2 * t, 2 * t + 1) if st < ST]

        @block.sync
        def _(sp):
            def load_chunk(n, buf):
                sp.dma_start(craw[:, buf], a["ctxT"][n]).then_inc(c_loaded[buf], 16)

            def load_queries(u, h):
                sp.dma_start(f32(qbd[:, h].rearrange("p x g n -> p (x g n)")), a["qbd_dram"][u]).then_inc(qbd_loaded[h], 16)

            def batch(b, last):
                for c in range(2 if last else 4):
                    sp.wait_ge(split_done, b * 4 + (c + 1))
                    load_chunk(b * 4 + (c + 2), c % 2)
                if not last:
                    for h in range(2):
                        sp.wait_ge(sc_full, b * 32 + 16 * (h + 1))
                        load_queries(b * 2 + (h + 2), h)

            for c in range(2):
                load_chunk(c, c)
            for h in range(2):
                load_queries(h, h)
            with sp.Fori(0, B - 1) as b:
                batch(b, False)
            batch(B - 1, True)

        @block.gpsimd
        def _(pool):
            def split(b, first):
                for c in range(NCH):
                    cols = slice(CW * c, CW * c + CW)
                    if c == 0 and not first:
                        pool.wait_ge(v_full, b * (2 * NV))
                    pool.wait_ge(c_loaded[c % 2], b * 32 + 16 * (c // 2 + 1))
                    nc.gpsimd.tensor_tensor(c_hi[:, :, cols], craw[:, c % 2], ones[:, 0:1].unsqueeze(2).to_broadcast([P, KD, CW]),
                                            ALU.mult).then_inc(split_hi, 1)
                    pool.wait_ge(split_hi, b * 4 + (c + 1))
                    nc.gpsimd.tensor_tensor(c_lo[:, :, cols], craw[:, c % 2], f32(c_hi[:, :, cols]),
                                            ALU.subtract).then_inc(split_done, 1)

            split(0, True)
            with pool.Fori(1, B) as b:
                split(b, False)

        @block.tensor
        def _(pe):
            def keys(b, h, n):
                c, m = n // 2, n % 2
                if h == 0 and m == 0:
                    pe.wait_ge(split_done, b * 4 + (c + 1))
                if n >= 4:
                    pe.wait_ge(k_lo_done, b * 16 + (8 * h + n - 3))
                f = slice(P * (2 * h + m), P * (2 * h + m) + P)
                for k in range(KD):
                    s = slice(CW * c, CW * c + CW)
                    ins = mm3(nc, ps[:, n % 4, 0:CW], wkv_hi[:, k, f], wkv_lo[:, k, f], c_hi[:, k, s], c_lo[:, k, s],
                              k == 0, k == KD - 1)
                ins.then_inc(k_full, 1)

            def values(b, h, v):
                if v == 2:
                    pe.wait_ge(o_done, b * 4 + (2 * h + 1))
                if v >= 4:
                    pe.wait_ge(v_lo_done, b * 14 + (7 * h + {4: 1, 5: 2, 6: 4}[v]))
                f = slice(D + 256 * h, D + 256 * h + 256)
                for st in tiles(v):
                    r = rows(st)
                    for k in range(KD):
                        s = slice(P * st, P * st + r)
                        ins = mm3(nc, ps[0:r, V_BANK[v], 256 * (st % 2):256 * (st % 2) + 256], c_hi[:, k, s],
                                  c_lo[:, k, s], wkv_hi[:, k, f], wkv_lo[:, k, f], k == 0, k == KD - 1)
                ins.then_inc(v_full, 1)

            def scores(b, h, p):
                g, j = p // 2, p % 2
                r = slice(64 * j, 64 * j + 64)
                if p == 0:
                    pe.wait_ge(k_lo_done, b * 16 + 8 * (h + 1))
                    pe.wait_ge(qbd_loaded[h], b * 16 + 16)
                for n, (s0, w, _) in enumerate(SC_CHUNKS):
                    if p >= 1 and n % 2 == 0:
                        pe.wait_ge(exp_done, b * 16 + (8 * h + 2 * (p - 1) + n // 2 + 1))
                    mm3(nc, ps[:, n, 0:w], qbd[r, h, 0, g], qbd[r, h, 1, g], kT_hi[r, g, s0:s0 + w],
                        kT_lo[r, g, s0:s0 + w], True, True).then_inc(sc_full, 1)

            def sums(b, h, g):
                if g == 0:
                    pe.wait_ge(v_lo_done, b * 14 + 7 * (h + 1))
                pe.wait_ge(diag_done, b * 8 + (4 * h + 2 * g + 2))
                for j in range(2):
                    nc.tensor.matmul(ps[:, 4 + g, 256 + P * j:256 + P * j + P], ones[:], diag[:, g, j], start=True, stop=True)

            def turn(b, h, g, t):
                n = 7 * g + t
                if n < 2:
                    pe.wait_ge(v_lo_done, b * 14 + (7 * h + 5 + n))
                else:
                    pe.wait_ge(pT_lo_done, b * 28 + (14 * h + n - 1))
                if t == 0:
                    pe.wait_ge(exp_done, b * 16 + (8 * h + 4 * g + 4))
                for st in tiles(t):
                    r = rows(st)
                    for j in range(2):
                        c = 256 * (st % 2) + P * j
                        ins = nc.tensor.transpose(ps[0:r, 6 + n % 2, c:c + P], prob[:, 2 * g + j, P * st:P * st + r], ident[:])
                ins.then_inc(pT_full, 1)

            def weigh(b, h, g, t):
                n = 7 * g + t
                pe.wait_ge(pT_lo_done, b * 28 + (14 * h + n + 1))
                for st in tiles(t):
                    r = rows(st)
                    s = slice(256 * (st % 2), 256 * (st % 2) + 256)
                    f = slice(P * g, P * g + P)
                    ins = mm3(nc, ps[:, 4 + g, 0:256], v_hi[0:r, st, f], v_lo[0:r, st, f], pT_hi[0:r, n % 2, s],
                              pT_lo[0:r, n % 2, s], st == 0, st == ST - 1)
                if t == NV - 1:
                    ins.then_inc(pv_full, 1)

            def unit(b, h, last):
                nb, nh = (b, 1) if h == 0 else (b + 1, 0)
                values(b, h, 0)
                scores(b, h, 0)
                values(b, h, 1)
                values(b, h, 2)
                scores(b, h, 1)
                for v in range(3, NV):
                    values(b, h, v)
                turn(b, h, 0, 0)
                scores(b, h, 2)
                for t in range(1, NV):
                    turn(b, h, 0, t)
                    if t == 1:
                        sums(b, h, 0)
                    if t == 3:
                        scores(b, h, 3)
                    weigh(b, h, 0, t - 1)
                turn(b, h, 1, 0)
                weigh(b, h, 0, NV - 1)
                sums(b, h, 1)
                if not last:
                    keys(nb, nh, 0)
                for t in range(1, NV):
                    turn(b, h, 1, t)
                    if not last:
                        keys(nb, nh, t)
                    weigh(b, h, 1, t - 1)
                if not last:
                    keys(nb, nh, 7)
                weigh(b, h, 1, NV - 1)

            for n in range(8):
                keys(0, 0, n)
            with pe.Fori(0, B - 1) as b:
                unit(b, 0, False)
                unit(b, 1, False)
            unit(B - 1, 0, False)
            unit(B - 1, 1, True)

        @block.scalar
        def _(act):
            def keys(b, h, n):
                c, m = n // 2, n % 2
                act.wait_ge(k_full, b * 16 + (8 * h + n + 1))
                nc.scalar.activation(kT_hi[:, m, CW * c:CW * c + CW], ps[:, n % 4, 0:CW], ACT.Identity,
                                     bias=bk[:, 2 * h + m:2 * h + m + 1]).then_inc(k_hi_done, 1)

            def values(b, h, v):
                act.wait_ge(v_full, b * 14 + (7 * h + v + 1))
                w, r = len(tiles(v)), rows(2 * v)
                nc.scalar.copy(v_hi[0:r, 2 * v:2 * v + w].rearrange("p a n -> p (a n)"),
                               ps[0:r, V_BANK[v], 0:256 * w]).then_inc(v_hi_done, 1)

            def exponentials(b, h, p):
                act.wait_ge(max_done, b * 8 + (4 * h + p + 1))
                for n, (s0, s1) in enumerate(((0, 1024), (1024, S))):
                    nc.scalar.activation(prob[:, p, s0:s1], sc[:, s0:s1], ACT.Exp, bias=nmax[:, p:p + 1],
                                         accum_out=psums[:, p, n:n + 1]).then_inc(exp_done, 1)

            def turned(b, h, g, t):
                n = 7 * g + t
                act.wait_ge(pT_full, b * 28 + (14 * h + n + 1))
                w, r = 256 * len(tiles(t)), rows(2 * t)
                nc.scalar.copy(pT_hi[0:r, n % 2, 0:w], ps[0:r, 6 + n % 2, 0:w]).then_inc(pT_hi_done, 1)

            def sums(b, h, g):
                act.wait_ge(pv_full, b * 4 + (2 * h + g + 1))
                nc.scalar.copy(rsb[:, g], ps[:, 4 + g, 256:512]).then_inc(rsb_done, 1)

            def unit(b, h, last):
                nb, nh = (b, 1) if h == 0 else (b + 1, 0)
                values(b, h, 0)
                exponentials(b, h, 0)
                values(b, h, 1)
                values(b, h, 2)
                exponentials(b, h, 1)
                for v in range(3, NV):
                    values(b, h, v)
                turned(b, h, 0, 0)
                turned(b, h, 0, 1)
                exponentials(b, h, 2)
                for t in range(2, NV):
                    turned(b, h, 0, t)
                    if t == 4:
                        exponentials(b, h, 3)
                turned(b, h, 1, 0)
                if not last:
                    keys(nb, nh, 0)
                sums(b, h, 0)
                for t in range(1, NV):
                    turned(b, h, 1, t)
                    if not last:
                        keys(nb, nh, t)
                if not last:
                    keys(nb, nh, 7)
                sums(b, h, 1)

            for n in range(8):
                keys(0, 0, n)
            with act.Fori(0, B - 1) as b:
                unit(b, 0, False)
                unit(b, 1, False)
            unit(B - 1, 0, False)
            unit(B - 1, 1, True)

        @block.vector
        def _(dve):
            def keys(b, h, n):
                c, m = n // 2, n % 2
                cols = slice(CW * c, CW * c + CW)
                dve.wait_ge(k_hi_done, b * 16 + (8 * h + n + 1))
                nc.vector.scalar_tensor_tensor(kT_lo[:, m, cols], ps[:, n % 4, 0:CW], bk[:, 2 * h + m:2 * h + m + 1],
                                               f32(kT_hi[:, m, cols]), ALU.add, ALU.subtract).then_inc(k_lo_done, 1)

            def values(b, h, v):
                w, r = len(tiles(v)), rows(2 * v)
                dve.wait_ge(v_hi_done, b * 14 + (7 * h + v + 1))
                nc.vector.tensor_tensor(v_lo[0:r, 2 * v:2 * v + w].rearrange("p a n -> p (a n)"),
                                        ps[0:r, V_BANK[v], 0:256 * w],
                                        f32(v_hi[0:r, 2 * v:2 * v + w].rearrange("p a n -> p (a n)")),
                                        ALU.subtract).then_inc(v_lo_done, 1)

            def maxima(b, h, p):
                for n, (s0, _, w) in enumerate(SC_CHUNKS):
                    dve.wait_ge(sc_full, b * 32 + (16 * h + 4 * p + n + 1))
                    nc.vector.tensor_reduce(pmax[:, p % 2, n:n + 1], ps[:, n, 0:w], AX.X, ALU.max).then_inc(pmax_done, 1)
                dve.wait_ge(pmax_done, b * 32 + (16 * h + 4 * p + 4))
                nc.vector.tensor_reduce(nmax[:, p:p + 1], pmax[:, p % 2], AX.X, ALU.max, negate=True).then_inc(max_done, 1)

            def sums(b, h, g):
                dve.wait_ge(exp_done, b * 16 + (8 * h + 4 * g + 4))
                nc.vector.tensor_tensor(rsum[:, g], psums[:, 2 * g:2 * g + 2, 0], psums[:, 2 * g:2 * g + 2, 1],
                                        ALU.add).then_inc(sum_step, 1)
                dve.wait_ge(sum_step, b * 8 + (4 * h + 2 * g + 1))
                nc.vector.reciprocal(rinv[:, g], rsum[:, g]).then_inc(sum_step, 1)
                dve.wait_ge(sum_step, b * 8 + (4 * h + 2 * g + 2))
                for j in range(2):
                    nc.vector.tensor_scalar(diag[:, g, j], ident[:], rinv[:, g, j:j + 1], None, ALU.mult).then_inc(diag_done, 1)

            def turned(b, h, g, t):
                n = 7 * g + t
                w, r = 256 * len(tiles(t)), rows(2 * t)
                dve.wait_ge(pT_hi_done, b * 28 + (14 * h + n + 1))
                nc.vector.tensor_tensor(pT_lo[0:r, n % 2, 0:w], ps[0:r, 6 + n % 2, 0:w], f32(pT_hi[0:r, n % 2, 0:w]),
                                        ALU.subtract).then_inc(pT_lo_done, 1)

            def output(b, h, g):
                dve.wait_ge(rsb_done, b * 4 + (2 * h + g + 1))
                for i in range(4):
                    q = slice(32 * i, 32 * i + 32)
                    c = slice(64 * i, 64 * i + 64)
                    ins = nc.vector.tensor_tensor(oT[q, 2 * h + g, bass.ds(b * L, L)], ps[q, 4 + g, c], rsb[q, g, c], ALU.mult)
                ins.then_inc(o_done, 1)

            def unit(b, h, last):
                nb, nh = (b, 1) if h == 0 else (b + 1, 0)
                values(b, h, 0)
                maxima(b, h, 0)
                values(b, h, 1)
                values(b, h, 2)
                maxima(b, h, 1)
                for v in range(3, NV):
                    values(b, h, v)
                sums(b, h, 0)
                turned(b, h, 0, 0)
                maxima(b, h, 2)
                for t in range(1, NV):
                    turned(b, h, 0, t)
                    if t == 3:
                        maxima(b, h, 3)
                turned(b, h, 1, 0)
                sums(b, h, 1)
                if not last:
                    keys(nb, nh, 0)
                output(b, h, 0)
                for t in range(1, NV):
                    turned(b, h, 1, t)
                    if not last:
                        keys(nb, nh, t)
                if not last:
                    keys(nb, nh, 7)
                output(b, h, 1)

            dve.sem_inc(o_done, 1)
            for n in range(8):
                keys(0, 0, n)
            with dve.Fori(0, B - 1) as b:
                unit(b, 0, False)
                unit(b, 1, False)
            unit(B - 1, 0, False)
            unit(B - 1, 1, True)


def normaliser(nc, sb, sem, name):
    stats, mv = sb(name + "_stats", [P, TT, 6]), sb(name + "_mv", [P, TT, 2])
    veps, std, rstd = (sb(f"{name}_{n}", [P, TT]) for n in ("veps", "std", "rstd"))
    step, std_done = sem(name + "_step"), sem(name + "_std_done")

    def on_vector(dve, src, dst, done, ready=None):
        for t in range(TT):
            if ready is not None:
                dve.wait_ge(ready, t + 1)
            ins = nc.vector.bn_stats(stats[:, t], src[:, t])
        ins.then_inc(step, 1)
        dve.wait_ge(step, 1)
        for t in range(TT):
            ins = nc.vector.bn_aggr(mv[:, t], stats[:, t])
        ins.then_inc(step, 1)
        dve.wait_ge(step, 2)
        nc.vector.tensor_scalar(veps[:], mv[:, :, 1], EPS, None, ALU.add).then_inc(step, 1)
        dve.wait_ge(std_done, 1)
        nc.vector.reciprocal(rstd[:], std[:]).then_inc(step, 1)
        dve.wait_ge(step, 4)
        for t in range(TT):
            nc.vector.tensor_scalar(dst[:, t], src[:, t], mv[:, t, 0:1], rstd[:, t:t + 1], ALU.subtract,
                                    ALU.mult).then_inc(done, 1)

    def on_scalar(act):
        act.wait_ge(step, 3)
        nc.scalar.activation(std[:], veps[:], ACT.Sqrt).then_inc(std_done, 1)

    return on_vector, on_scalar


def head_attention(nc, a, keep):
    ident, tokA, tokB = keep["ident"], keep["oT"], keep["x"]
    NR, NS, NP = 2, 3, 4
    QR = 4
    NQ, NA = 2 * H2 // QR, H2 // QR
    PW = QR * 2 * H2 * D2
    with ExitStack() as ctx:
        def sb(name, shape, dt=F32):
            return ctx.enter_context(nc.sbuf_tensor(name, shape, dt))

        def sem(name):
            return ctx.enter_context(nc.semaphore(name))

        raw = sb("h_raw", [P, NR, KD, D])
        w_hi = [sb(f"h_w_hi{i}", [P, KD, D], F32R) for i in range(NS)]
        w_lo = [sb(f"h_w_lo{i}", [P, KD, D], F32R) for i in range(NS)]
        row = sb("h_row", [P, 2, D])
        cols = sb("h_cols", [P, 2, KD])
        lam4 = sb("h_lam4", [P, 4, D2])
        lprod, lsum, lexp = sb("h_lprod", [P, 2, D2]), sb("h_lsum", [P, 2]), sb("h_lexp", [P, 2])
        ldif, lam = sb("h_ldif", [P, 1]), sb("h_lam", [P, 1])
        a_hi, a_lo = sb("h_a_hi", [P, KD, T], F32R), sb("h_a_lo", [P, KD, T], F32R)
        hT = sb("h_hT", [P, KD, T])
        q = sb("h_q", [P, TT, 2 * H2, D2])
        k = sb("h_k", [P, TT, 2 * H2, D2])
        v = sb("h_v", [P, TT, 2 * D2, H2])
        prod = sb("h_prod", [P, NP, PW])
        att = sb("h_att", [P, 2, 2 * H2, 2 * H2])
        z1, z2 = sb("h_z1", [P, 4 * H2 * H2]), sb("h_z2", [P, 4 * H2 * H2])
        ex = sb("h_ex", [P, 2 * H2, 2 * H2])
        rmax, rsum = sb("h_rmax", [P, 2 * H2]), sb("h_rsum", [P, 2 * H2])
        rinv, rlam = sb("h_rinv", [P, 2 * H2]), sb("h_rlam", [P, H2])
        w0, w1, att2 = (sb(f"h_{n}", [P, H2, H2]) for n in ("w0", "w1", "att2"))
        o = sb("h_o", [P, 2, H2, 2 * D2])
        sq = sb("h_sq", [P, H2, 2 * D2])
        ms, mse, rms, rrms = (sb(f"h_{n}", [P, H2]) for n in ("ms", "mse", "rms", "rrms"))
        on = sb("h_on", [P, 2, D])
        ps = ctx.enter_context(nc.psum_tensor("ps_h", [P, 8, 512], F32))

        w_loaded = [sem(f"h_w_loaded{i}") for i in range(NR)]
        x_loaded, c_loaded = sem("h_x_loaded"), sem("h_c_loaded")
        whi_done, wlo_done = sem("h_whi_done"), sem("h_wlo_done")
        o_hi_done, o_lo_done = sem("h_o_hi_done"), sem("h_o_lo_done")
        xb_done, x1_full, x1_done = sem("h_xb_done"), sem("h_x1_full"), sem("h_x1_done")
        y_done, yn_done, yb_done = sem("h_y_done"), sem("h_yn_done"), sem("h_yb_done")
        tr_full, hT_done, h_hi_done, h_lo_done = (sem(f"h_{n}") for n in ("tr_full", "hT_done", "h_hi_done", "h_lo_done"))
        qkv_full, qkv_done = sem("h_qkv_full"), sem("h_qkv_done")
        lam_step, lexp_done = sem("h_lam_step"), sem("h_lexp_done")
        prod_done, red_done = sem("h_prod_done"), sem("h_red_done")
        z_done, zsum_done = sem("h_z_done"), sem("h_zsum_done")
        rmax_done, sub_done, exp_done = sem("h_rmax_done"), sem("h_sub_done"), sem("h_exp_done")
        rsum_step, w01_done, att2_done = sem("h_rsum_step"), sem("h_w01_done"), sem("h_att2_done")
        sq_done, ms_step, rms_done, on_done = sem("h_sq_done"), sem("h_ms_step"), sem("h_rms_done"), sem("h_on_done")
        aT_full, aT_hi_done, aT_lo_done = sem("h_aT_full"), sem("h_aT_hi_done"), sem("h_aT_lo_done")
        src_full, conn_done = sem("h_src_full"), sem("h_conn_done")
        norm1, norm1_act = normaliser(nc, sb, sem, "h_n1")
        norm2, norm2_act = normaliser(nc, sb, sem, "h_n2")

        block = ctx.enter_context(nc.Block())

        order, at_qk, at_av = [], {}, {}
        for t in range(TT + 1):
            for i in range(NQ if t < TT else 0):
                at_qk[t, i] = len(order)
                order.append(("qk", t, i))
            for i in range(NA if t else 0):
                at_av[t - 1, i] = len(order)
                order.append(("av", t - 1, i))

        @block.sync
        def _(sp):
            def load(s):
                if s >= NR:
                    sp.wait_ge(wlo_done, s - NR + 1)
                sp.dma_start(raw[:, s % NR], a["slabs"][s]).then_inc(w_loaded[s % NR], 16)
            load(0)
            sp.dma_start(tokB[:], a["x"].rearrange("(t p) d -> p t d", p=P)).then_inc(x_loaded, 16)
            sp.dma_start(row[:], a["rows"][0:2].partition_broadcast(P)).then_inc(x_loaded, 16)
            load(1)
            sp.dma_start(cols[:], a["ln1"]).then_inc(c_loaded, 16)
            sp.dma_start(lam4[:], a["lambdas"].partition_broadcast(P)).then_inc(c_loaded, 16)
            for s in range(2, 5):
                load(s)

        @block.gpsimd
        def _(pool):
            def low(s):
                pool.wait_ge(whi_done, s + 1)
                if s == 4:
                    pool.wait_ge(wlo_done, 4)
                nc.gpsimd.tensor_tensor(w_lo[s % NS][:], raw[:, s % NR], f32(w_hi[s % NS][:]), ALU.subtract).then_inc(wlo_done, 1)

            def product(n):
                kind, t, i = order[n]
                if n >= NP:
                    pool.wait_ge(red_done, n - NP + 1)
                r = slice(QR * i, QR * i + QR)
                if kind == "qk":
                    out = prod[:, n % NP].rearrange("p (a b d) -> p a b d", a=QR, b=2 * H2)
                    shape = [P, QR, 2 * H2, D2]
                    pool.wait_ge(qkv_done, 3 * t + 2)
                    nc.gpsimd.tensor_tensor(out, q[:, t, r].unsqueeze(2).to_broadcast(shape),
                                            k[:, t].unsqueeze(1).to_broadcast(shape), ALU.mult).then_inc(prod_done, 1)
                else:
                    out = prod[:, n % NP].rearrange("p (a d h) -> p a d h", a=QR, d=2 * D2)
                    shape = [P, QR, 2 * D2, H2]
                    pool.wait_ge(att2_done, t + 1)
                    nc.gpsimd.tensor_tensor(out, att2[:, r].unsqueeze(2).to_broadcast(shape),
                                            v[:, t].unsqueeze(1).to_broadcast(shape), ALU.mult).then_inc(prod_done, 1)

            def add_z(t):
                pool.wait_ge(z_done, 2 * t + 2)
                nc.gpsimd.tensor_tensor(att[:, t % 2].rearrange("p a b -> p (a b)"), z1[:], z2[:], ALU.add).then_inc(zsum_done, 1)

            def subtract_max(t):
                pool.wait_ge(rmax_done, t + 1)
                nc.gpsimd.tensor_tensor(att[:, t % 2], att[:, t % 2], rmax[:].unsqueeze(2).to_broadcast([P, 2 * H2, 2 * H2]),
                                        ALU.subtract).then_inc(sub_done, 1)

            def weights(t):
                pool.wait_ge(rsum_step, 3 * t + 3)
                if t:
                    pool.wait_ge(att2_done, t)
                nc.gpsimd.tensor_tensor(w0[:], ex[:, 0:H2, 0:H2], rinv[:, 0:H2].unsqueeze(2).to_broadcast([P, H2, H2]),
                                        ALU.mult).then_inc(w01_done, 1)
                nc.gpsimd.tensor_tensor(w1[:], ex[:, H2:, H2:], rlam[:].unsqueeze(2).to_broadcast([P, H2, H2]),
                                        ALU.mult).then_inc(w01_done, 1)
                pool.wait_ge(w01_done, 2 * t + 2)
                if t:
                    pool.wait_ge(prod_done, at_av[t - 1, NA - 1] + 1)
                nc.gpsimd.tensor_tensor(att2[:], w0[:], w1[:], ALU.subtract).then_inc(att2_done, 1)

            def square(t):
                pool.wait_ge(red_done, at_av[t, NA - 1] + 1)
                if t:
                    pool.wait_ge(ms_step, 3 * t)
                nc.gpsimd.tensor_tensor(sq[:], o[:, t % 2], o[:, t % 2], ALU.mult).then_inc(sq_done, 1)

            def scale(t):
                pool.wait_ge(ms_step, 3 * t + 3)
                if t >= 2:
                    pool.wait_ge(aT_full, t - 1)
                nc.gpsimd.tensor_tensor(on[:, t % 2].rearrange("p (a d) -> p a d", a=H2), o[:, t % 2],
                                        rrms[:].unsqueeze(2).to_broadcast([P, H2, 2 * D2]), ALU.mult).then_inc(on_done, 1)

            low(0)
            pool.wait_ge(x_loaded, 32)
            nc.gpsimd.tensor_tensor(tokB[:], tokB[:], row[:, 0].unsqueeze(1).to_broadcast([P, TT, D]), ALU.add).then_inc(xb_done, 1)
            for s in range(1, 4):
                low(s)
            pool.wait_ge(yn_done, TT)
            nc.gpsimd.tensor_tensor(tokA[:], tokA[:], row[:, 1].unsqueeze(1).to_broadcast([P, TT, D]), ALU.add).then_inc(yb_done, 1)
            for t in range(TT + 1):
                for i in range(NQ if t < TT else 0):
                    product(at_qk[t, i])
                    if t and i == 1:
                        add_z(t - 1)
                    if t and i == 3:
                        subtract_max(t - 1)
                    if t >= 2 and i == 4:
                        scale(t - 2)
                if t == TT:
                    add_z(t - 1)
                    scale(t - 2)
                    subtract_max(t - 1)
                if t:
                    weights(t - 1)
                    for i in range(NA):
                        product(at_av[t - 1, i])
                    square(t - 1)
                if t == 1:
                    low(4)
            scale(TT - 1)

        @block.scalar
        def _(act):
            def high(s):
                act.wait_ge(w_loaded[s % NR], 16 * (s // NR + 1))
                if s == 3:
                    act.wait_ge(x1_full, TT)
                if s == 4:
                    act.wait_ge(qkv_full, 3 * TT)
                nc.scalar.copy(w_hi[s % NS][:], raw[:, s % NR]).then_inc(whi_done, 1)

            for g in range(KD):
                nc.scalar.activation(a_hi[:, g], tokA[:, g], ACT.Identity, bias=keep["bv"][:, g:g + 1]).then_inc(o_hi_done, 1)
            for s in range(3):
                high(s)
            norm1_act(act)
            high(3)
            norm2_act(act)
            act.wait_ge(c_loaded, 32)
            act.wait_ge(tr_full, KD)
            for g in range(KD):
                nc.scalar.activation(hT[:, g], ps[:, 4 + g], ACT.Identity, bias=cols[:, 1, g:g + 1],
                                     scale=cols[:, 0, g:g + 1]).then_inc(hT_done, 1)
            act.wait_ge(lam_step, 2)
            nc.scalar.activation(lexp[:], lsum[:], ACT.Exp).then_inc(lexp_done, 1)
            for n in range(3 * TT):
                t, w = n // 3, n % 3
                act.wait_ge(qkv_full, n + 1)
                if w < 2:
                    nc.scalar.mul((q, k)[w][:, t].rearrange("p (c h) d -> p h d c", c=2),
                                  ps[:, n % 8].rearrange("p (h d c) -> p h d c", h=H2, c=2),
                                  (float(D2) ** -0.5, 1.0)[w]).then_inc(qkv_done, 1)
                else:
                    nc.scalar.copy(v[:, t].rearrange("p d h -> p h d"),
                                   ps[:, n % 8].rearrange("p (h d) -> p h d", h=H2)).then_inc(qkv_done, 1)
            high(4)
            for t in range(TT):
                act.wait_ge(sub_done, t + 1)
                nc.scalar.activation(ex[:].rearrange("p a b -> p (a b)"), att[:, t % 2].rearrange("p a b -> p (a b)"),
                                     ACT.Exp).then_inc(exp_done, 1)
                act.wait_ge(ms_step, 3 * t + 2)
                nc.scalar.activation(rms[:], mse[:], ACT.Sqrt).then_inc(rms_done, 1)
                act.wait_ge(aT_full, t + 1)
                nc.scalar.copy(a_hi[:, :, P * t:P * t + P], ps[:, t].rearrange("p (k n) -> p k n", k=KD)).then_inc(aT_hi_done, 1)

        @block.vector
        def _(dve):
            def reduce(n):
                kind, t, i = order[n]
                r = slice(QR * i, QR * i + QR)
                out = att[:, t % 2, r] if kind == "qk" else o[:, t % 2, r]
                if kind == "av" and i == 0 and t >= 2:
                    dve.wait_ge(on_done, t - 1)
                dve.wait_ge(prod_done, n + 1)
                nc.vector.tensor_reduce(out, prod[:, n % NP].rearrange("p (a b d) -> p a b d", a=QR, d=D2), AX.X,
                                        ALU.add).then_inc(red_done, 1)

            def clean(t):
                x = att[:, t % 2].rearrange("p a b -> p (a b)")
                dve.wait_ge(red_done, at_qk[t, NQ - 1] + 1)
                nc.vector.tensor_scalar(z1[:], x, 0.0, -FMAX, ALU.min, ALU.max).then_inc(z_done, 1)
                nc.vector.tensor_scalar(z2[:], x, 0.0, FMAX, ALU.max, ALU.min).then_inc(z_done, 1)

            def row_max(t):
                dve.wait_ge(zsum_done, t + 1)
                nc.vector.tensor_reduce(rmax[:], att[:, t % 2], AX.X, ALU.max).then_inc(rmax_done, 1)

            def row_sum(t):
                dve.wait_ge(exp_done, t + 1)
                nc.vector.tensor_reduce(rsum[:], ex[:], AX.X, ALU.add).then_inc(rsum_step, 1)
                dve.wait_ge(rsum_step, 3 * t + 1)
                nc.vector.reciprocal(rinv[:], rsum[:]).then_inc(rsum_step, 1)
                dve.wait_ge(rsum_step, 3 * t + 2)
                nc.vector.tensor_scalar(rlam[:], rinv[:, H2:], lam[:], None, ALU.mult).then_inc(rsum_step, 1)

            def mean_square(t):
                dve.wait_ge(sq_done, t + 1)
                nc.vector.tensor_reduce(ms[:], sq[:], AX.X, ALU.add).then_inc(ms_step, 1)
                dve.wait_ge(ms_step, 3 * t + 1)
                c = (1.0 - LAMBDA_INIT) ** -2
                nc.vector.tensor_scalar(mse[:], ms[:], c / (2 * D2), c * EPS, ALU.mult, ALU.add).then_inc(ms_step, 1)
                dve.wait_ge(rms_done, t + 1)
                nc.vector.reciprocal(rrms[:], rms[:]).then_inc(ms_step, 1)

            def attended_low(t):
                dve.wait_ge(aT_hi_done, t + 1)
                s = slice(P * t, P * t + P)
                nc.vector.tensor_tensor(a_lo[:, :, s], ps[:, t].rearrange("p (k n) -> p k n", k=KD), f32(a_hi[:, :, s]),
                                        ALU.subtract).then_inc(aT_lo_done, 1)

            def skip(t):
                dve.wait_ge(src_full, t + 1)
                nc.vector.tensor_tensor(tokA[:, t], ps[:, 4 + t], tokA[:, t], ALU.add).then_inc(conn_done, 1)

            for g in range(KD):
                dve.wait_ge(o_hi_done, g + 1)
                nc.vector.scalar_tensor_tensor(a_lo[:, g], tokA[:, g], keep["bv"][:, g:g + 1], f32(a_hi[:, g]), ALU.add,
                                               ALU.subtract).then_inc(o_lo_done, 1)
            dve.wait_ge(c_loaded, 32)
            nc.vector.tensor_tensor(lprod[:], lam4[:, 0:2], lam4[:, 2:4], ALU.mult).then_inc(lam_step, 1)
            dve.wait_ge(lam_step, 1)
            nc.vector.tensor_reduce(lsum[:], lprod[:], AX.X, ALU.add).then_inc(lam_step, 1)
            dve.wait_ge(xb_done, 1)
            for t in range(TT):
                dve.wait_ge(x1_full, t + 1)
                nc.vector.tensor_tensor(tokB[:, t], ps[:, t], tokB[:, t], ALU.add).then_inc(x1_done, 1)
            norm1(dve, tokB, tokA, y_done, x1_done)
            norm2(dve, tokA, hT, yn_done, y_done)
            for g in range(KD):
                dve.wait_ge(hT_done, g + 1)
                nc.vector.tensor_copy(a_hi[:, g], hT[:, g]).then_inc(h_hi_done, 1)
                dve.wait_ge(h_hi_done, g + 1)
                nc.vector.tensor_tensor(a_lo[:, g], hT[:, g], f32(a_hi[:, g]), ALU.subtract).then_inc(h_lo_done, 1)
            dve.wait_ge(lexp_done, 1)
            nc.vector.tensor_tensor(ldif[:], lexp[:, 0:1], lexp[:, 1:2], ALU.subtract).then_inc(lam_step, 1)
            dve.wait_ge(lam_step, 3)
            nc.vector.tensor_scalar(lam[:], ldif[:], LAMBDA_INIT, None, ALU.add).then_inc(lam_step, 1)
            dve.wait_ge(lam_step, 4)
            dve.wait_ge(yb_done, 1)
            for t in range(TT + 1):
                for i in range(NQ if t < TT else 0):
                    reduce(at_qk[t, i])
                    if t and i == 2:
                        row_max(t - 1)
                    if t and i == 5:
                        row_sum(t - 1)
                if t == TT:
                    row_max(t - 1)
                    row_sum(t - 1)
                if t < TT:
                    clean(t)
                for i in range(NA if t else 0):
                    reduce(at_av[t - 1, i])
                if t:
                    mean_square(t - 1)
                if t >= 2:
                    attended_low(t - 2)
                    skip(t - 2)
            attended_low(TT - 1)
            skip(TT - 1)

        @block.tensor
        def _(pe):
            pe.wait_ge(wlo_done, 1)
            for t in range(TT):
                for g in range(KD):
                    if t == 0:
                        pe.wait_ge(o_lo_done, g + 1)
                    ins = mm3(nc, ps[:, t], a_hi[:, g, P * t:P * t + P], a_lo[:, g, P * t:P * t + P], w_hi[0][:, g], w_lo[0][:, g],
                              g == 0, g == KD - 1)
                ins.then_inc(x1_full, 1)
            for g in range(KD):
                for t in range(TT):
                    if g == 0:
                        pe.wait_ge(yn_done, t + 1)
                    ins = nc.tensor.transpose(ps[:, 4 + g, P * t:P * t + P], hT[:, t, P * g:P * g + P], ident[:])
                ins.then_inc(tr_full, 1)
            pe.wait_ge(h_lo_done, KD)
            pe.wait_ge(x1_done, TT)
            for n in range(3 * TT):
                t, w = n // 3, n % 3
                s = 1 + w
                if t == 0:
                    pe.wait_ge(wlo_done, s + 1)
                if n >= 8:
                    pe.wait_ge(qkv_done, n - 7)
                for g in range(KD):
                    ins = mm3(nc, ps[:, n % 8], a_hi[:, g, P * t:P * t + P], a_lo[:, g, P * t:P * t + P], w_hi[s % NS][:, g],
                              w_lo[s % NS][:, g], g == 0, g == KD - 1)
                ins.then_inc(qkv_full, 1)
            pe.wait_ge(qkv_done, 3 * TT)
            pe.wait_ge(wlo_done, 5)
            for t in range(TT):
                pe.wait_ge(on_done, t + 1)
                for g in range(KD):
                    ins = nc.tensor.transpose(ps[:, t, P * g:P * g + P], on[:, t % 2, P * g:P * g + P], ident[:])
                ins.then_inc(aT_full, 1)
                pe.wait_ge(aT_lo_done, t + 1)
                for g in range(KD):
                    ins = mm3(nc, ps[:, 4 + t], a_hi[:, g, P * t:P * t + P], a_lo[:, g, P * t:P * t + P], w_hi[4 % NS][:, g],
                              w_lo[4 % NS][:, g], g == 0, g == KD - 1)
                ins.then_inc(src_full, 1)


def feed_forward(nc, a, keep):
    ident, tokA, tokB = keep["ident"], keep["oT"], keep["x"]
    NR, NS, NF, NSLAB, FT = 3, 5, 3, 8, FF // P
    with ExitStack() as ctx:
        def sb(name, shape, dt=F32):
            return ctx.enter_context(nc.sbuf_tensor(name, shape, dt))

        def sem(name):
            return ctx.enter_context(nc.semaphore(name))

        raw = sb("f_raw", [P, NR, KD, D])
        w_hi = [sb(f"f_w_hi{i}", [P, KD, D], F32R) for i in range(NS)]
        w_lo = [sb(f"f_w_lo{i}", [P, KD, D], F32R) for i in range(NS)]
        row = sb("f_row", [P, D])
        cols = sb("f_cols", [P, 2, KD])
        b1 = sb("f_b1", [P, FT])
        a_hi, a_lo = sb("f_a_hi", [P, KD, T], F32R), sb("f_a_lo", [P, KD, T], F32R)
        cn = sb("f_cn", [P, TT, D])
        hT = sb("f_hT", [P, KD, T])
        fT = sb("f_fT", [P, NF, T])
        f_hi, f_lo = sb("f_f_hi", [P, NF, T], F32R), sb("f_f_lo", [P, NF, T], F32R)
        ps = ctx.enter_context(nc.psum_tensor("ps_f", [P, 8, 512], F32))

        w_loaded = [sem(f"f_w_loaded{i}") for i in range(NR)]
        c_loaded, b_loaded = sem("f_c_loaded"), sem("f_b_loaded")
        whi_done, wlo_done = sem("f_whi_done"), sem("f_wlo_done")
        cn_done, skip_done = sem("f_cn_done"), sem("f_skip_done")
        tr_full, hT_done, h_hi_done, h_lo_done = (sem(f"f_{n}") for n in ("tr_full", "hT_done", "h_hi_done", "h_lo_done"))
        up_full, f_done, f_hi_done, f_lo_done = (sem(f"f_{n}") for n in ("up_full", "f_done", "f_hi_done", "f_lo_done"))
        down_full, x2_done = sem("f_down_full"), sem("f_x2_done")
        norm, norm_act = normaliser(nc, sb, sem, "f_n")

        block = ctx.enter_context(nc.Block())
        behind = {5: 4, 6: 6, 7: 8}

        @block.sync
        def _(sp):
            for s in range(NSLAB):
                if s >= NR:
                    sp.wait_ge(wlo_done, s - NR + 1)
                sp.dma_start(raw[:, s % NR], a["slabs"][5 + s]).then_inc(w_loaded[s % NR], 16)
                if s == 0:
                    sp.dma_start(cols[:], a["ln2"]).then_inc(c_loaded, 16)
                    sp.dma_start(b1[:], a["b1"]).then_inc(c_loaded, 16)
                    sp.dma_start(row[:], a["rows"][2].partition_broadcast(P)).then_inc(b_loaded, 16)

        @block.gpsimd
        def _(pool):
            def low(s):
                pool.wait_ge(whi_done, s + 1)
                nc.gpsimd.tensor_tensor(w_lo[s % NS][:], raw[:, s % NR], f32(w_hi[s % NS][:]), ALU.subtract).then_inc(wlo_done, 1)

            for s in range(NS):
                low(s)
            pool.wait_ge(b_loaded, 16)
            pool.wait_ge(cn_done, TT)
            nc.gpsimd.tensor_tensor(tokA[:], tokA[:], row[:].unsqueeze(1).to_broadcast([P, TT, D]), ALU.add).then_inc(skip_done, 1)
            pool.wait_ge(skip_done, 1)
            nc.gpsimd.tensor_tensor(tokB[:], tokA[:], tokB[:], ALU.add).then_inc(skip_done, 1)
            for f in range(FT):
                pool.wait_ge(f_hi_done, f + 1)
                nc.gpsimd.tensor_tensor(f_lo[:, f % NF], fT[:, f % NF], f32(f_hi[:, f % NF]), ALU.subtract).then_inc(f_lo_done, 1)
                for s in [s for s, after in behind.items() if after == f]:
                    low(s)

        @block.scalar
        def _(act):
            def high(s):
                act.wait_ge(w_loaded[s % NR], 16 * (s // NR + 1))
                if s >= NS:
                    used = s - NS
                    act.wait_ge(down_full if used % 2 else up_full, 4 * (used // 2) + 4)
                nc.scalar.copy(w_hi[s % NS][:], raw[:, s % NR]).then_inc(whi_done, 1)

            high(0)
            norm_act(act)
            high(1)
            act.wait_ge(c_loaded, 32)
            for g in range(KD):
                act.wait_ge(tr_full, g + 1)
                nc.scalar.activation(hT[:, g], ps[:, g], ACT.Identity, bias=cols[:, 1, g:g + 1],
                                     scale=cols[:, 0, g:g + 1]).then_inc(hT_done, 1)
            for s in range(2, NS):
                high(s)
            for f in range(FT):
                act.wait_ge(up_full, f + 1)
                if f >= NF:
                    act.wait_ge(f_lo_done, f - NF + 1)
                nc.scalar.activation(fT[:, f % NF], ps[:, 4 + f % 4], ACT.Relu, bias=b1[:, f:f + 1]).then_inc(f_done, 1)
                for s in [s for s, after in behind.items() if after == f]:
                    high(s)

        @block.vector
        def _(dve):
            norm(dve, tokA, cn, cn_done)
            for g in range(KD):
                dve.wait_ge(hT_done, g + 1)
                nc.vector.tensor_copy(a_hi[:, g], hT[:, g]).then_inc(h_hi_done, 1)
                dve.wait_ge(h_hi_done, g + 1)
                nc.vector.tensor_tensor(a_lo[:, g], hT[:, g], f32(a_hi[:, g]), ALU.subtract).then_inc(h_lo_done, 1)
            for f in range(FT):
                dve.wait_ge(f_done, f + 1)
                if f >= NF:
                    dve.wait_ge(down_full, f - NF + 1)
                nc.vector.tensor_copy(f_hi[:, f % NF], fT[:, f % NF]).then_inc(f_hi_done, 1)
            dve.wait_ge(skip_done, 2)
            dve.wait_ge(down_full, FT)
            for t in range(TT):
                nc.vector.tensor_tensor(tokB[:, t], ps[:, t], tokB[:, t], ALU.add).then_inc(x2_done, 1)

        @block.tensor
        def _(pe):
            for g in range(KD):
                for t in range(TT):
                    if g == 0:
                        pe.wait_ge(cn_done, t + 1)
                    ins = nc.tensor.transpose(ps[:, g, P * t:P * t + P], cn[:, t, P * g:P * g + P], ident[:])
                ins.then_inc(tr_full, 1)
            pe.wait_ge(h_lo_done, KD)

            def up(f):
                s = 2 * (f // 4)
                if f % 4 == 0:
                    pe.wait_ge(wlo_done, s + 1)
                if f >= 4:
                    pe.wait_ge(f_done, f - 3)
                c = slice(P * (f % 4), P * (f % 4) + P)
                for g in range(KD):
                    ins = mm3(nc, ps[:, 4 + f % 4], w_hi[s % NS][:, g, c], w_lo[s % NS][:, g, c], a_hi[:, g], a_lo[:, g],
                              g == 0, g == KD - 1)
                ins.then_inc(up_full, 1)

            def down(f):
                s = 2 * (f // 4) + 1
                if f % 4 == 0:
                    pe.wait_ge(wlo_done, s + 1)
                pe.wait_ge(f_lo_done, f + 1)
                for t in range(TT):
                    c = slice(P * t, P * t + P)
                    ins = mm3(nc, ps[:, t], f_hi[:, f % NF, c], f_lo[:, f % NF, c], w_hi[s % NS][:, f % 4], w_lo[s % NS][:, f % 4],
                              f == 0, f == FT - 1)
                ins.then_inc(down_full, 1)

            for f in range(FT + 2):
                if f < FT:
                    up(f)
                if f >= 2:
                    down(f - 2)


def route(nc, a, keep):
    ident, x2, m_hi, m_lo = keep["ident"], keep["x"], keep["m_hi"], keep["m_lo"]
    with ExitStack() as ctx:
        def sb(name, shape, dt=F32):
            return ctx.enter_context(nc.sbuf_tensor(name, shape, dt))

        def sem(name):
            return ctx.enter_context(nc.semaphore(name))

        xm = sb("r_xm", [P, TT, D])
        graw = sb("r_graw", [P, KD, E])
        g_hi, g_lo = sb("r_g_hi", [P, KD, E], F32R), sb("r_g_lo", [P, KD, E], F32R)
        bias = sb("r_bias", [P, E])
        score, sfc = sb("r_score", [P, TT, E]), sb("r_sfc", [P, TT, E])
        gmax, gtop = sb("r_gmax", [P, TT, NG]), sb("r_gtop", [P, TT, 8])
        ggt, geq, gcum, gsel = (sb(f"r_{n}", [P, TT, NG]) for n in ("ggt", "geq", "gcum", "gsel"))
        gleft = sb("r_gleft", [P, TT])
        masked, etop = sb("r_masked", [P, TT, E]), sb("r_etop", [P, TT, 8])
        egt, eeq, ecum, esel = (sb(f"r_{n}", [P, TT, E]) for n in ("egt", "eeq", "ecum", "esel"))
        eleft = sb("r_eleft", [P, TT])
        weight, wsum, winv = sb("r_weight", [P, TT, E]), sb("r_wsum", [P, TT]), sb("r_winv", [P, TT])
        comb = sb("r_comb", [P, TT, NX])
        combT = sb("r_combT", [NX, T])
        onesE = sb("r_ones", [P, E])
        ps = ctx.enter_context(nc.psum_tensor("ps_r", [P, 8, 512], F32))

        g_loaded, b_loaded = sem("r_g_loaded"), sem("r_b_loaded")
        ghi_done, glo_done = sem("r_ghi_done"), sem("r_glo_done")
        xm_done, tr_full, m_hi_done, m_lo_done = sem("r_xm_done"), sem("r_tr_full"), sem("r_m_hi_done"), sem("r_m_lo_done")
        logit_full, score_done = sem("r_logit_full"), sem("r_score_done")
        step, comb_done, combT_full, combT_done, stored = (sem(f"r_{n}") for n in ("step", "comb_done", "combT_full", "combT_done", "stored"))
        norm, norm_act = normaliser(nc, sb, sem, "r_n")

        block = ctx.enter_context(nc.Block())

        @block.sync
        def _(sp):
            sp.dma_start(graw[:], a["gateT"]).then_inc(g_loaded, 16)
            sp.dma_start(bias[:], a["e_bias"].partition_broadcast(P)).then_inc(b_loaded, 16)
            sp.wait_ge(combT_done, 1)
            sp.dma_start(a["comb_dram"], combT[:]).then_inc(stored, 16)
            sp.wait_ge(stored, 16)

        @block.gpsimd
        def _(pool):
            pool.wait_ge(ghi_done, 1)
            nc.gpsimd.tensor_tensor(g_lo[:], graw[:], f32(g_hi[:]), ALU.subtract).then_inc(glo_done, 1)

        @block.scalar
        def _(act):
            act.wait_ge(g_loaded, 16)
            nc.scalar.copy(g_hi[:], graw[:]).then_inc(ghi_done, 1)
            norm_act(act)
            for g in range(KD):
                act.wait_ge(tr_full, g + 1)
                nc.scalar.copy(m_hi[:, g], ps[:, g]).then_inc(m_hi_done, 1)
            act.wait_ge(logit_full, 1)
            nc.scalar.activation(score[:].rearrange("p t e -> p (t e)"), ps[:, 4, 0:TT * E], ACT.Sigmoid).then_inc(score_done, 1)

        @block.vector
        def _(dve):
            steps = [0]

            def link(ins):
                steps[0] += 1
                ins.then_inc(step, 1)
                dve.wait_ge(step, steps[0])

            def first(n, values, top, gt, eq, cum, left, sel, width):
                for t in range(TT):
                    ins = nc.vector.max(top[:, t], values[:, t])
                link(ins)
                level = top[:, :, n - 1:n].to_broadcast([P, TT, width])
                nc.vector.tensor_tensor(gt[:], values[:], level, ALU.is_gt)
                link(nc.vector.tensor_tensor(eq[:], values[:], level, ALU.is_equal))
                for t in range(TT):
                    nc.vector.tensor_tensor_scan(cum[:, t], onesE[:, 0:width], eq[:, t], 0.0, ALU.mult, ALU.add)
                link(nc.vector.tensor_reduce(left[:], gt[:], AX.X, ALU.add))
                link(nc.vector.tensor_scalar(left[:], left[:], -1.0, float(n), ALU.mult, ALU.add))
                link(nc.vector.tensor_tensor(cum[:], cum[:], left[:].unsqueeze(2).to_broadcast([P, TT, width]), ALU.is_le))
                link(nc.vector.tensor_tensor(eq[:], eq[:], cum[:], ALU.mult))
                link(nc.vector.tensor_tensor(sel[:], gt[:], eq[:], ALU.add))

            nc.vector.memset(onesE[:], 1.0)
            nc.vector.memset(comb[:, :, E:NX], 1.0)
            norm(dve, x2, xm, xm_done)
            for g in range(KD):
                dve.wait_ge(m_hi_done, g + 1)
                nc.vector.tensor_tensor(m_lo[:, g], ps[:, g], f32(m_hi[:, g]), ALU.subtract).then_inc(m_lo_done, 1)
            dve.wait_ge(b_loaded, 16)
            dve.wait_ge(score_done, 1)
            link(nc.vector.tensor_tensor(sfc[:], score[:], bias[:].unsqueeze(1).to_broadcast([P, TT, E]), ALU.add))
            link(nc.vector.tensor_reduce(gmax[:], sfc[:].rearrange("p t (g s) -> p t g s", g=NG), AX.X, ALU.max))
            first(TOPKG, gmax, gtop, ggt, geq, gcum, gleft, gsel, NG)
            for t in range(TT):
                ins = nc.vector.tensor_tensor(masked[:, t].rearrange("p (g s) -> p g s", g=NG),
                                              sfc[:, t].rearrange("p (g s) -> p g s", g=NG),
                                              gsel[:, t].unsqueeze(2).to_broadcast([P, NG, GS]), ALU.mult)
            link(ins)
            first(TOPK, masked, etop, egt, eeq, ecum, eleft, esel, E)
            link(nc.vector.tensor_tensor(weight[:], score[:], esel[:], ALU.mult))
            link(nc.vector.tensor_reduce(wsum[:], weight[:], AX.X, ALU.add))
            link(nc.vector.tensor_scalar(wsum[:], wsum[:], 1e-20, None, ALU.add))
            link(nc.vector.reciprocal(winv[:], wsum[:]))
            link(nc.vector.tensor_scalar(winv[:], winv[:], SCALE, None, ALU.mult))
            nc.vector.tensor_tensor(comb[:, :, 0:E], weight[:], winv[:].unsqueeze(2).to_broadcast([P, TT, E]),
                                    ALU.mult).then_inc(comb_done, 1)
            dve.wait_ge(combT_full, 1)
            nc.vector.tensor_copy(combT[:], ps[0:NX, 5, :]).then_inc(combT_done, 1)

        @block.tensor
        def _(pe):
            for g in range(KD):
                for t in range(TT):
                    if g == 0:
                        pe.wait_ge(xm_done, t + 1)
                    ins = nc.tensor.transpose(ps[:, g, P * t:P * t + P], xm[:, t, P * g:P * g + P], ident[:])
                ins.then_inc(tr_full, 1)
            pe.wait_ge(glo_done, 1)
            pe.wait_ge(m_lo_done, KD)
            for t in range(TT):
                c = slice(P * t, P * t + P)
                for g in range(KD):
                    ins = mm3(nc, ps[:, 4, E * t:E * t + E], m_hi[:, g, c], m_lo[:, g, c], g_hi[:, g], g_lo[:, g],
                              g == 0, g == KD - 1)
            ins.then_inc(logit_full, 1)
            pe.wait_ge(comb_done, 1)
            for t in range(TT):
                ins = nc.tensor.transpose(ps[0:NX, 5, P * t:P * t + P], comb[:, t], ident[:])
            ins.then_inc(combT_full, 1)


def experts(nc, a, keep):
    x2, m_hi, m_lo = keep["x"], keep["m_hi"], keep["m_lo"]
    WG, WE = KD * 2 * I, KD * 2 * I + (I // P) * D
    with ExitStack() as ctx:
        def sb(name, shape, dt=F32):
            return ctx.enter_context(nc.sbuf_tensor(name, shape, dt))

        def sem(name):
            return ctx.enter_context(nc.semaphore(name))

        raw = sb("e_raw", [P, 2, WE])
        w_hi, w_lo = sb("e_w_hi", [P, 2, WE], F32R), sb("e_w_lo", [P, 2, WE], F32R)
        cb = sb("e_cb", [P, 2, T])
        sg = sb("e_sg", [P, 2, T])
        t1, hid = sb("e_t1", [P, 2, T]), sb("e_hid", [P, 2, T])
        h_hi, h_lo = sb("e_h_hi", [P, 2, 2, T], F32R), sb("e_h_lo", [P, 2, 2, T], F32R)
        y = sb("e_y", [P, TT, D])
        ps = ctx.enter_context(nc.psum_tensor("ps_e", [P, 8, 512], F32))

        w_loaded = [sem(f"e_w_loaded{i}") for i in range(2)]
        c_loaded = [sem(f"e_c_loaded{i}") for i in range(2)]
        whi_done, wlo_done = sem("e_whi_done"), sem("e_wlo_done")
        up_full, sg_done, sc_done, t1_done, hid_done, h_hi_done, h_lo_done = (
            sem(f"e_{n}") for n in ("up_full", "sg_done", "sc_done", "t1_done", "hid_done", "h_hi_done", "h_lo_done"))
        down_full, y_done, stored = sem("e_down_full"), sem("e_y_done"), sem("e_stored")

        block = ctx.enter_context(nc.Block())

        def gu(w, s):
            return w[:, s, 0:WG].rearrange("p (k n) -> p k n", k=KD)

        def dn(w, s):
            return w[:, s, WG:WE].rearrange("p (k n) -> p k n", k=I // P)

        @block.sync
        def _(sp):
            def load(e, s, first):
                if not first:
                    sp.wait_ge(wlo_done, e - 1)
                sp.dma_start(raw[:, s], a["experts"][e]).then_inc(w_loaded[s], 16)
                if not first:
                    sp.wait_ge(sc_done, e * 2 - 2)
                sp.dma_start(cb[:, s], a["comb_dram"][e].partition_broadcast(P)).then_inc(c_loaded[s], 16)

            for e in range(2):
                load(e, e, True)
            with sp.Fori(0, (NX - 2) // 2) as i:
                for s in range(2):
                    load(i * 2 + (s + 2), s, False)
            for t in range(TT):
                sp.wait_ge(y_done, t + 1)
                sp.dma_start(a["out"][P * t:P * t + P], y[:, t]).then_inc(stored, 16)
            sp.wait_ge(stored, 16 * TT)

        @block.scalar
        def _(act):
            def split(i, s, first):
                act.wait_ge(w_loaded[s], i * 16 + 16)
                if not first:
                    act.wait_ge(down_full, i * 2 + (s - 1))
                nc.scalar.copy(w_hi[:, s], raw[:, s]).then_inc(whi_done, 1)

            def gates(i, s):
                for m in range(2):
                    act.wait_ge(up_full, i * 4 + (2 * s + m + 1))
                    nc.scalar.activation(sg[:, m], ps[:, 4 + 2 * m], ACT.Sigmoid).then_inc(sg_done, 1)

            split(0, 0, True)
            split(0, 1, True)
            with act.Fori(0, NX // 2 - 1) as i:
                gates(i, 0)
                split(i + 1, 0, False)
                gates(i, 1)
                split(i + 1, 1, False)
            gates(NX // 2 - 1, 0)
            gates(NX // 2 - 1, 1)

        @block.gpsimd
        def _(pool):
            def split(i, s):
                pool.wait_ge(whi_done, i * 2 + (s + 1))
                nc.gpsimd.tensor_tensor(w_lo[:, s], raw[:, s], f32(w_hi[:, s]), ALU.subtract).then_inc(wlo_done, 1)

            def hidden(i, s):
                for m in range(2):
                    n = 2 * s + m + 1
                    if m == 0:
                        pool.wait_ge(c_loaded[s], i * 16 + 16)
                    pool.wait_ge(sg_done, i * 4 + n)
                    nc.gpsimd.tensor_tensor(sg[:, m], sg[:, m], cb[:, s], ALU.mult).then_inc(sc_done, 1)
                for m in range(2):
                    pool.wait_ge(h_hi_done, i * 4 + (2 * s + m + 1))
                    nc.gpsimd.tensor_tensor(h_lo[:, s, m], hid[:, m], f32(h_hi[:, s, m]), ALU.subtract).then_inc(h_lo_done, 1)

            split(0, 0)
            split(0, 1)
            with pool.Fori(0, NX // 2 - 1) as i:
                hidden(i, 0)
                split(i + 1, 0)
                hidden(i, 1)
                split(i + 1, 1)
            hidden(NX // 2 - 1, 0)
            hidden(NX // 2 - 1, 1)

        @block.vector
        def _(dve):
            def hidden(i, s):
                for m in range(2):
                    n = 2 * s + m + 1
                    dve.wait_ge(sc_done, i * 4 + n)
                    nc.vector.tensor_tensor(t1[:, m], ps[:, 4 + 2 * m], sg[:, m], ALU.mult).then_inc(t1_done, 1)
                    dve.wait_ge(t1_done, i * 4 + n)
                    nc.vector.tensor_tensor(hid[:, m], ps[:, 5 + 2 * m], t1[:, m], ALU.mult).then_inc(hid_done, 1)
                    dve.wait_ge(hid_done, i * 4 + n)
                    nc.vector.tensor_copy(h_hi[:, s, m], hid[:, m]).then_inc(h_hi_done, 1)

            with dve.Fori(0, NX // 2) as i:
                hidden(i, 0)
                hidden(i, 1)
            dve.wait_ge(down_full, NX)
            for t in range(TT):
                nc.vector.tensor_tensor(y[:, t], ps[:, t], x2[:, t], ALU.add).then_inc(y_done, 1)

        @block.tensor
        def _(pe):
            def up(i, s, first=False):
                pe.wait_ge(wlo_done, i * 2 + (s + 1))
                for m in range(2):
                    if not first:
                        pe.wait_ge(hid_done, i * 4 + (2 * s + m - 1))
                    for u in range(2):
                        c = slice(I * u + P * m, I * u + P * m + P)
                        for g in range(KD):
                            ins = mm3(nc, ps[:, 4 + 2 * m + u], gu(w_hi, s)[:, g, c], gu(w_lo, s)[:, g, c], m_hi[:, g], m_lo[:, g],
                                      g == 0, g == KD - 1)
                    ins.then_inc(up_full, 1)

            def down(i, s, first=False, last=False):
                for m in range(2):
                    pe.wait_ge(h_lo_done, i * 4 + (2 * s + m + 1))
                    for t in range(TT):
                        c = slice(P * t, P * t + P)
                        ins = mm3(nc, ps[:, t], h_hi[:, s, m, c], h_lo[:, s, m, c], dn(w_hi, s)[:, m], dn(w_lo, s)[:, m],
                                  first and m == 0, last and m == 1)
                ins.then_inc(down_full, 1)

            up(0, 0, first=True)
            up(0, 1)
            down(0, 0, first=True)
            with pe.Fori(0, NX // 2 - 1) as i:
                up(i + 1, 0)
                down(i, 1)
                up(i + 1, 1)
                down(i + 1, 0)
            down(NX // 2 - 1, 1, last=True)


INPUTS = ("x", "identity", "b_Q", "b_K", "b_V", "w_qkv", "ctxT", "slabs", "rows", "ln1", "ln2", "b1", "lambdas",
          "gateT", "e_bias", "experts")


def build(nc, a):
    a["qbd_dram"] = nc.dram_tensor("qbd_dram", (2 * B, P, 512), F32, kind="Internal").ap()
    a["comb_dram"] = nc.dram_tensor("comb_dram", (NX, T), F32, kind="Internal").ap()
    with ExitStack() as ctx:
        def sb(stack, name, shape, dt=F32):
            return stack.enter_context(nc.sbuf_tensor(name, shape, dt))

        keep = {"ident": sb(ctx, "ident", [P, P]), "ones": sb(ctx, "ones", [P, P]), "bk": sb(ctx, "bk", [P, KD]),
                "bv": sb(ctx, "bv", [P, KD]), "oT": sb(ctx, "oT", [P, KD, T])}
        with ExitStack() as own:
            keep["wkv_hi"] = sb(own, "wkv_hi", [P, KD, 2 * D], F32R)
            keep["wkv_lo"] = sb(own, "wkv_lo", [P, KD, 2 * D], F32R)
            queries(nc, a, keep)
            cross_attention(nc, a, keep)
        keep["x"] = sb(ctx, "x_tok", [P, TT, D])
        head_attention(nc, a, keep)
        feed_forward(nc, a, keep)
        keep["m_hi"], keep["m_lo"] = sb(ctx, "m_hi", [P, KD, T], F32R), sb(ctx, "m_lo", [P, KD, T], F32R)
        route(nc, a, keep)
        experts(nc, a, keep)


def _by_rows(w):
    return np.ascontiguousarray(w.reshape(-1, P, w.shape[1]).transpose(1, 0, 2))


def _by_column(v):
    return np.ascontiguousarray(v.reshape(-1, P).T)


def _expert(gate_up, down):
    return np.concatenate([_by_rows(gate_up).reshape(P, -1), _by_rows(down).reshape(P, -1)], 1)


def _layout(i):
    x, h, f = (lambda n: i["L0_xattn_" + n]), (lambda n: i["L0_attn_" + n]), (lambda n: i["L0_ffn_" + n])
    ctx = np.zeros((B, SP_, D), np.float32)
    ctx[:, :S] = i["ctx_1024"]
    slabs = [x("W_O"), h("Wq").T, h("Wk").T, h("Wv").T, h("Wo").T]
    for n in range(FF // D):
        slabs += [h("W1").T[:, D * n:D * n + D], h("W2").T[D * n:D * n + D]]
    gu, dn = f("experts_gate_up").transpose(0, 2, 1), f("experts_down").transpose(0, 2, 1)
    sg, su, sd = f("shared_gate_w").T, f("shared_up_w").T, f("shared_down_w").T
    ex = [_expert(gu[e], dn[e]) for e in range(E)]
    for n in range(2):
        s = slice(I * n, I * n + I)
        ex.append(_expert(np.concatenate([sg[:, s], su[:, s]], 1), sd[s]))
    return {
        "x": i["x"].reshape(T, D),
        "identity": np.eye(P, dtype=np.float32),
        "b_Q": _by_column(x("b_Q")), "b_K": _by_column(x("b_K")), "b_V": _by_column(x("b_V")),
        "w_qkv": np.stack([_by_rows(x("W_" + n)) for n in "QKV"]),
        "ctxT": np.ascontiguousarray(ctx.reshape(B, NCH, CW, KD, P).transpose(0, 1, 4, 3, 2)).reshape(B * NCH, P, KD, CW),
        "slabs": np.stack([_by_rows(w) for w in slabs]),
        "rows": np.stack([x("b_O"), h("bo"), h("b2")]),
        "ln1": np.stack([_by_column(h("ln1_g")), _by_column(h("ln1_b"))], 1),
        "ln2": np.stack([_by_column(h("ln2_g")), _by_column(h("ln2_b"))], 1),
        "b1": _by_column(h("b1")),
        "lambdas": np.stack([h("lq1"), h("lq2"), h("lk1"), h("lk2")]),
        "gateT": _by_rows(f("gate_weight").T),
        "e_bias": f("e_score_correction_bias"),
        "experts": np.stack(ex),
    }


def kernel(**inputs):
    import concourse.bacc as bacc
    from concourse.bass_utils import run_bass_kernel_spmd

    arrays = _layout({n: np.asarray(v) for n, v in inputs.items()})
    nc = bacc.Bacc("TRN2", target_bir_lowering=False, num_devices=1)
    args = {n: nc.dram_tensor(n, arrays[n].shape, F32, kind="ExternalInput").ap() for n in INPUTS}
    args["out"] = nc.dram_tensor("out", (T, D), F32, kind="ExternalOutput").ap()
    build(nc, args)
    result = run_bass_kernel_spmd(nc, [{n: np.ascontiguousarray(v) for n, v in arrays.items()}], core_ids=[0])
    return result.results[0]["out"].reshape(B, L, D)
```

```python
from contextlib import ExitStack

import numpy as np

import concourse.bass as bass
from concourse import mybir

F32 = mybir.dt.float32
F32R = mybir.dt.float32r
ALU = mybir.AluOpType
ACT = mybir.ActivationFunctionType
AX = mybir.AxisListType

P = 128
B, L, D = 8, 64, 512
S = 1601
T = B * L
TT = T // P
KD = D // P
EPS = 1e-5

NH, DK = 16, 32
NCH = 4
CW = 402
SP_ = NCH * CW
ST = -(-S // P)
LAST = S - (ST - 1) * P
NV = -(-ST // 2)
SC_CHUNKS = [(0, 512, 512), (512, 512, 512), (1024, 512, 512), (1536, 66, 65)]
V_BANK = [6, 7, 4, 5, 6, 7, 5]

H2, D2 = 16, 16
FF = 2048
LAMBDA_INIT = 0.8 - 0.6 * float(np.exp(-0.3 * 1.0))
FMAX = float(np.finfo(np.float32).max)

E, I = 32, 256
NG, GS = 8, 4
TOPK, TOPKG = 6, 4
SCALE = 2.5
U = 3
MAXB = E + (T * TOPK - E) // P
NBLK = -(-MAXB // U) * U + 2 * U
NF = 6


def f32(ap):
    return ap.bitcast(F32)


def mm3(nc, out, a_hi, a_lo, b_hi, b_lo, start, stop):
    nc.tensor.matmul(out, a_hi, b_hi, start=start, stop=False)
    nc.tensor.matmul(out, a_hi, b_lo, start=False, stop=False)
    return nc.tensor.matmul(out, a_lo, b_hi, start=False, stop=stop)


def queries(nc, a, keep):
    ident, wkv_hi, wkv_lo = keep["ident"], keep["wkv_hi"], keep["wkv_lo"]
    signals = []
    with ExitStack() as ctx:
        def sb(name, shape, dt=F32):
            return ctx.enter_context(nc.sbuf_tensor(name, shape, dt))

        def sem(name):
            signals.append(nc.alloc_semaphore(name))
            return signals[-1]

        x_sb = sb("x_sb", [P, TT, D])
        stats = sb("stats", [P, TT, 6])
        mv = sb("mv", [P, TT, 2])
        veps = sb("veps", [P, TT])
        std = sb("std", [P, TT])
        rstd = sb("rstd", [P, TT])
        xn = sb("xn", [P, TT, D])
        xnT_hi = sb("xnT_hi", [P, KD, T], F32R)
        xnT_lo = sb("xnT_lo", [P, KD, T], F32R)
        wraw = sb("wraw", [P, 3, KD, D])
        wq_hi = sb("wq_hi", [P, KD, D], F32R)
        wq_lo = sb("wq_lo", [P, KD, D], F32R)
        bq = sb("bq", [P, KD])
        bqs = sb("bqs", [P, KD])
        qf = sb("qf", [P, KD, T])
        qbd = sb("qbd_all", [P, B, 2, 2, 2, P], F32R)
        ps = ctx.enter_context(nc.psum_tensor("ps_q", [P, 8, 512], F32))

        x_loaded = sem("q_x_loaded")
        w_loaded = [sem(f"q_w_loaded{i}") for i in range(3)]
        c_loaded = sem("q_c_loaded")
        bq_loaded = sem("q_bq_loaded")
        dve_step = sem("q_dve_step")
        std_done = sem("q_std_done")
        xn_done = sem("q_xn_done")
        tr_full = sem("q_tr_full")
        xT_hi_done = sem("q_xT_hi_done")
        xT_lo_done = sem("q_xT_lo_done")
        w_hi_done = sem("q_w_hi_done")
        kv_hi_done = sem("q_kv_hi_done")
        w_lo_done = sem("q_w_lo_done")
        bqs_done = sem("q_bqs_done")
        q_full = sem("q_full")
        qf_done = sem("q_qf_done")
        zero_done = sem("q_zero_done")
        q_hi_done = sem("q_hi_done")
        q_lo_done = sem("q_lo_done")
        q_stored = sem("q_stored")

        block = ctx.enter_context(nc.Block())
        scale = float(DK) ** -0.5

        def diagonal(i):
            return slice(32 * i, 32 * i + 32), slice(64 * (i % 2), 64 * (i % 2) + 64)

        @block.sync
        def _(sp):
            sp.dma_start(x_sb[:], a["x"].rearrange("(t p) d -> p t d", p=P)).then_inc(x_loaded, 16)
            sp.dma_start(ident[:], a["identity"]).then_inc(c_loaded, 16)
            sp.dma_start(bq[:], a["b_Q"]).then_inc(bq_loaded, 16)
            sp.dma_start(keep["bk"][:], a["b_K"]).then_inc(c_loaded, 16)
            sp.dma_start(keep["bv"][:], a["b_V"]).then_inc(c_loaded, 16)
            for i in range(3):
                sp.dma_start(wraw[:, i], a["w_qkv"][i]).then_inc(w_loaded[i], 16)
            for h in range(2):
                sp.wait_ge(q_hi_done, 8 * h + 8)
                sp.wait_ge(q_lo_done, 8 * h + 8)
                sp.dma_start(a["qbd_dram"].rearrange("(b h) p n -> p b h n", h=2)[:, :, h],
                             f32(qbd[:, :, h].rearrange("p b x g n -> p b (x g n)"))).then_inc(q_stored, 16)
            sp.wait_ge(q_stored, 32)
            sp.wait_ge(c_loaded, 48)

        @block.gpsimd
        def _(pool):
            nc.gpsimd.memset(f32(qbd[:].rearrange("p b h x g n -> p (b h x g n)")), 0.0).then_inc(zero_done, 1)
            pool.wait_ge(w_hi_done, 1)
            nc.gpsimd.tensor_tensor(wq_lo[:], wraw[:, 0], f32(wq_hi[:]), ALU.subtract).then_inc(w_lo_done, 1)
            for i in range(2):
                c = slice(D * i, D * i + D)
                pool.wait_ge(kv_hi_done, i + 1)
                nc.gpsimd.tensor_tensor(wkv_lo[:, :, c], wraw[:, i + 1], f32(wkv_hi[:, :, c]), ALU.subtract).then_inc(w_lo_done, 1)

        @block.scalar
        def _(act):
            act.wait_ge(w_loaded[0], 16)
            nc.scalar.copy(wq_hi[:], wraw[:, 0]).then_inc(w_hi_done, 1)
            act.wait_ge(dve_step, 3)
            nc.scalar.activation(std[:], veps[:], ACT.Sqrt).then_inc(std_done, 1)
            for k in range(KD):
                act.wait_ge(tr_full, k + 1)
                nc.scalar.copy(xnT_hi[:, k], ps[:, k]).then_inc(xT_hi_done, 1)
            act.wait_ge(bqs_done, 1)
            for G in range(KD):
                act.wait_ge(q_full, G + 1)
                nc.scalar.activation(qf[:, G], ps[:, 4 + G], ACT.Identity, bias=bqs[:, G:G + 1],
                                     scale=scale).then_inc(qf_done, 1)
                act.wait_ge(qf_done, G + 1)
                if G == 0:
                    act.wait_ge(zero_done, 1)
                for i in range(4):
                    q, block_cols = diagonal(i)
                    nc.scalar.copy(qbd[q, :, G // 2, 0, G % 2, block_cols],
                                   qf[q, G, :].rearrange("p (b l) -> p b l", b=B)).then_inc(q_hi_done, 1)

        @block.vector
        def _(dve):
            nc.vector.memset(keep["ones"][:], 1.0)
            dve.wait_ge(bq_loaded, 16)
            nc.vector.tensor_scalar(bqs[:], bq[:], scale, None, ALU.mult).then_inc(bqs_done, 1)
            dve.wait_ge(x_loaded, 16)
            for t in range(TT):
                ins = nc.vector.bn_stats(stats[:, t], x_sb[:, t])
            ins.then_inc(dve_step, 1)
            dve.wait_ge(dve_step, 1)
            for t in range(TT):
                ins = nc.vector.bn_aggr(mv[:, t], stats[:, t])
            ins.then_inc(dve_step, 1)
            dve.wait_ge(dve_step, 2)
            nc.vector.tensor_scalar(veps[:], mv[:, :, 1], EPS, None, ALU.add).then_inc(dve_step, 1)
            dve.wait_ge(std_done, 1)
            nc.vector.reciprocal(rstd[:], std[:]).then_inc(dve_step, 1)
            dve.wait_ge(dve_step, 4)
            for t in range(TT):
                nc.vector.tensor_scalar(xn[:, t], x_sb[:, t], mv[:, t, 0:1], rstd[:, t:t + 1], ALU.subtract,
                                        ALU.mult).then_inc(xn_done, 1)
            for k in range(KD):
                dve.wait_ge(xT_hi_done, k + 1)
                nc.vector.tensor_tensor(xnT_lo[:, k], ps[:, k], f32(xnT_hi[:, k]), ALU.subtract).then_inc(xT_lo_done, 1)
            for i in range(2):
                dve.wait_ge(w_loaded[i + 1], 16)
                nc.vector.tensor_copy(wkv_hi[:, :, D * i:D * (i + 1)], wraw[:, i + 1]).then_inc(kv_hi_done, 1)
            for G in range(KD):
                for i in range(4):
                    q, block_cols = diagonal(i)
                    dve.wait_ge(q_hi_done, 4 * G + i + 1)
                    nc.vector.tensor_tensor(qbd[q, :, G // 2, 1, G % 2, block_cols], qf[q, G, :].rearrange("p (b l) -> p b l", b=B),
                                            f32(qbd[q, :, G // 2, 0, G % 2, block_cols]), ALU.subtract).then_inc(q_lo_done, 1)

        @block.tensor
        def _(pe):
            pe.wait_ge(c_loaded, 48)
            for k in range(KD):
                for t in range(TT):
                    if k == 0:
                        pe.wait_ge(xn_done, t + 1)
                    ins = nc.tensor.transpose(ps[:, k, P * t:P * t + P], xn[:, t, P * k:P * k + P], ident[:])
                ins.then_inc(tr_full, 1)
            pe.wait_ge(w_lo_done, 1)
            for G in range(KD):
                for k in range(KD):
                    if G == 0:
                        pe.wait_ge(xT_lo_done, k + 1)
                    ins = mm3(nc, ps[:, 4 + G], wq_hi[:, k, P * G:P * G + P], wq_lo[:, k, P * G:P * G + P],
                              xnT_hi[:, k], xnT_lo[:, k], k == 0, k == KD - 1)
                ins.then_inc(q_full, 1)
    nc.clear_and_free_semaphores(signals)
    nc.all_engine_barrier()


def cross_attention(nc, a, keep):
    ident, ones, wkv_hi, wkv_lo, bk, oT = (keep[n] for n in ("ident", "ones", "wkv_hi", "wkv_lo", "bk", "oT"))
    with ExitStack() as ctx:
        def sb(name, shape, dt=F32):
            return ctx.enter_context(nc.sbuf_tensor(name, shape, dt))

        def sem(name):
            return ctx.enter_context(nc.semaphore(name))

        craw = sb("craw", [P, 2, KD, CW])
        c_hi = sb("c_hi", [P, KD, SP_], F32R)
        c_lo = sb("c_lo", [P, KD, SP_], F32R)
        kT_hi = sb("kT_hi", [P, 2, SP_], F32R)
        kT_lo = sb("kT_lo", [P, 2, SP_], F32R)
        v_hi = sb("v_hi", [P, ST, 256], F32R)
        v_lo = sb("v_lo", [P, ST, 256], F32R)
        qbd = sb("qbd", [P, 2, 2, 2, P], F32R)
        prob = sb("prob", [P, 4, S])
        pT_hi = sb("pT_hi", [P, 2, 512], F32R)
        pT_lo = sb("pT_lo", [P, 2, 512], F32R)
        pmax = sb("pmax", [P, 2, 4])
        nmax = sb("nmax", [P, 4])
        psums = sb("psums", [P, 4, 2])
        rsum = sb("rsum", [P, 2, 2])
        rinv = sb("rinv", [P, 2, 2])
        diag = sb("diag", [P, 2, 2, P])
        rsb = sb("rsb", [P, 2, 256])
        ps = ctx.enter_context(nc.psum_tensor("ps_x", [P, 8, 512], F32))
        sc = ps[:, 0:4, :].rearrange("p a n -> p (a n)")

        c_loaded = [sem(f"x_c_loaded{i}") for i in range(2)]
        qbd_loaded = [sem(f"x_qbd_loaded{i}") for i in range(2)]
        split_hi = sem("x_split_hi")
        split_done = sem("x_split_done")
        k_full, k_hi_done, k_lo_done = sem("x_k_full"), sem("x_k_hi_done"), sem("x_k_lo_done")
        v_full, v_hi_done, v_lo_done = sem("x_v_full"), sem("x_v_hi_done"), sem("x_v_lo_done")
        sc_full = sem("x_sc_full")
        pmax_done, max_done = sem("x_pmax_done"), sem("x_max_done")
        exp_done = sem("x_exp_done")
        sum_step, diag_done = sem("x_sum_step"), sem("x_diag_done")
        pT_full, pT_hi_done, pT_lo_done = sem("x_pT_full"), sem("x_pT_hi_done"), sem("x_pT_lo_done")
        pv_full, rsb_done, o_done = sem("x_pv_full"), sem("x_rsb_done"), sem("x_o_done")

        block = ctx.enter_context(nc.Block())

        def rows(st):
            return P if st < ST - 1 else LAST

        def tiles(t):
            return [st for st in (2 * t, 2 * t + 1) if st < ST]

        KEYS_AT = {(0, 4): 0, (0, 5): 1, (0, 6): 2, (1, 0): 3, (1, 1): 4, (1, 3): 5, (1, 5): 6, (1, 6): 7}

        @block.sync
        def _(sp):
            def load_chunk(n, buf):
                sp.dma_start(craw[:, buf], a["ctxT"][n]).then_inc(c_loaded[buf], 16)

            def load_queries(u, h):
                sp.dma_start(f32(qbd[:, h].rearrange("p x g n -> p (x g n)")), a["qbd_dram"][u]).then_inc(qbd_loaded[h], 16)

            def batch(b, last):
                for c in range(2 if last else 4):
                    sp.wait_ge(split_done, b * 4 + (c + 1))
                    load_chunk(b * 4 + (c + 2), c % 2)
                if not last:
                    for h in range(2):
                        sp.wait_ge(sc_full, b * 32 + 16 * (h + 1))
                        load_queries(b * 2 + (h + 2), h)

            for c in range(2):
                load_chunk(c, c)
            for h in range(2):
                load_queries(h, h)
            with sp.Fori(0, B - 1) as b:
                batch(b, False)
            batch(B - 1, True)

        @block.gpsimd
        def _(pool):
            def split(b, first):
                for c in range(NCH):
                    cols = slice(CW * c, CW * c + CW)
                    if c == 0 and not first:
                        pool.wait_ge(v_full, b * (2 * NV))
                    pool.wait_ge(c_loaded[c % 2], b * 32 + 16 * (c // 2 + 1))
                    nc.gpsimd.tensor_tensor(c_hi[:, :, cols], craw[:, c % 2], ones[:, 0:1].unsqueeze(2).to_broadcast([P, KD, CW]),
                                            ALU.mult).then_inc(split_hi, 1)
                    pool.wait_ge(split_hi, b * 4 + (c + 1))
                    nc.gpsimd.tensor_tensor(c_lo[:, :, cols], craw[:, c % 2], f32(c_hi[:, :, cols]),
                                            ALU.subtract).then_inc(split_done, 1)

            split(0, True)
            with pool.Fori(1, B) as b:
                split(b, False)

        @block.tensor
        def _(pe):
            def keys(b, h, n, unit_before=None):
                c, m = n // 2, n % 2
                if h == 0 and m == 0:
                    pe.wait_ge(split_done, b * 4 + (c + 1))
                if n >= 4:
                    pe.wait_ge(k_lo_done, b * 16 + (8 * h + n - 3))
                elif n % 2 == 0 and unit_before is not None:
                    ub, uh = unit_before
                    pe.wait_ge(exp_done, ub * 16 + (8 * uh + 7 + n // 2))
                f = slice(P * (2 * h + m), P * (2 * h + m) + P)
                for k in range(KD):
                    s = slice(CW * c, CW * c + CW)
                    ins = mm3(nc, ps[:, n % 4, 0:CW], wkv_hi[:, k, f], wkv_lo[:, k, f], c_hi[:, k, s], c_lo[:, k, s],
                              k == 0, k == KD - 1)
                ins.then_inc(k_full, 1)

            def values(b, h, v):
                if v == 2:
                    pe.wait_ge(o_done, b * 4 + (2 * h + 1))
                if v >= 4:
                    pe.wait_ge(v_lo_done, b * 14 + (7 * h + {4: 1, 5: 2, 6: 4}[v]))
                f = slice(D + 256 * h, D + 256 * h + 256)
                for st in tiles(v):
                    r = rows(st)
                    for k in range(KD):
                        s = slice(P * st, P * st + r)
                        ins = mm3(nc, ps[0:r, V_BANK[v], 256 * (st % 2):256 * (st % 2) + 256], c_hi[:, k, s],
                                  c_lo[:, k, s], wkv_hi[:, k, f], wkv_lo[:, k, f], k == 0, k == KD - 1)
                ins.then_inc(v_full, 1)

            def scores(b, h, p):
                g, j = p // 2, p % 2
                r = slice(64 * j, 64 * j + 64)
                if p == 0:
                    pe.wait_ge(k_lo_done, b * 16 + 8 * (h + 1))
                    pe.wait_ge(qbd_loaded[h], b * 16 + 16)
                for n, (s0, w, _) in enumerate(SC_CHUNKS):
                    if p >= 1 and n % 2 == 0:
                        pe.wait_ge(exp_done, b * 16 + (8 * h + 2 * (p - 1) + n // 2 + 1))
                    mm3(nc, ps[:, n, 0:w], qbd[r, h, 0, g], qbd[r, h, 1, g], kT_hi[r, g, s0:s0 + w],
                        kT_lo[r, g, s0:s0 + w], True, True).then_inc(sc_full, 1)

            def sums(b, h, g):
                if g == 0:
                    pe.wait_ge(v_lo_done, b * 14 + 7 * (h + 1))
                pe.wait_ge(diag_done, b * 8 + (4 * h + 2 * g + 2))
                for j in range(2):
                    nc.tensor.matmul(ps[:, 4 + g, 256 + P * j:256 + P * j + P], ones[:], diag[:, g, j], start=True, stop=True)

            def turn(b, h, g, t):
                n = 7 * g + t
                if n < 2:
                    pe.wait_ge(v_lo_done, b * 14 + (7 * h + 5 + n))
                else:
                    pe.wait_ge(pT_lo_done, b * 28 + (14 * h + n - 1))
                if t == 0:
                    pe.wait_ge(exp_done, b * 16 + (8 * h + 4 * g + 4))
                for st in tiles(t):
                    r = rows(st)
                    for j in range(2):
                        c = 256 * (st % 2) + P * j
                        ins = nc.tensor.transpose(ps[0:r, 6 + n % 2, c:c + P], prob[:, 2 * g + j, P * st:P * st + r], ident[:])
                ins.then_inc(pT_full, 1)

            def weigh(b, h, g, t):
                n = 7 * g + t
                pe.wait_ge(pT_lo_done, b * 28 + (14 * h + n + 1))
                for st in tiles(t):
                    r = rows(st)
                    s = slice(256 * (st % 2), 256 * (st % 2) + 256)
                    f = slice(P * g, P * g + P)
                    ins = mm3(nc, ps[:, 4 + g, 0:256], v_hi[0:r, st, f], v_lo[0:r, st, f], pT_hi[0:r, n % 2, s],
                              pT_lo[0:r, n % 2, s], st == 0, st == ST - 1)
                if t == NV - 1:
                    ins.then_inc(pv_full, 1)

            def unit(b, h, last):
                nb, nh = (b, 1) if h == 0 else (b + 1, 0)

                def next_keys(g, t):
                    if not last and (g, t) in KEYS_AT:
                        keys(nb, nh, KEYS_AT[g, t], (b, h))

                values(b, h, 0)
                scores(b, h, 0)
                values(b, h, 1)
                values(b, h, 2)
                scores(b, h, 1)
                values(b, h, 3)
                values(b, h, 4)
                scores(b, h, 2)
                for v in range(5, NV):
                    values(b, h, v)
                turn(b, h, 0, 0)
                scores(b, h, 3)
                for t in range(1, NV):
                    turn(b, h, 0, t)
                    if t == 1:
                        sums(b, h, 0)
                    next_keys(0, t)
                    weigh(b, h, 0, t - 1)
                turn(b, h, 1, 0)
                next_keys(1, 0)
                weigh(b, h, 0, NV - 1)
                sums(b, h, 1)
                for t in range(1, NV):
                    turn(b, h, 1, t)
                    if t < NV - 1:
                        next_keys(1, t)
                    weigh(b, h, 1, t - 1)
                next_keys(1, NV - 1)
                weigh(b, h, 1, NV - 1)

            for n in range(8):
                keys(0, 0, n)
            with pe.Fori(0, B - 1) as b:
                unit(b, 0, False)
                unit(b, 1, False)
            unit(B - 1, 0, False)
            unit(B - 1, 1, True)

        @block.scalar
        def _(act):
            def keys(b, h, n):
                c, m = n // 2, n % 2
                act.wait_ge(k_full, b * 16 + (8 * h + n + 1))
                nc.scalar.activation(kT_hi[:, m, CW * c:CW * c + CW], ps[:, n % 4, 0:CW], ACT.Identity,
                                     bias=bk[:, 2 * h + m:2 * h + m + 1]).then_inc(k_hi_done, 1)

            def values(b, h, v):
                act.wait_ge(v_full, b * 14 + (7 * h + v + 1))
                w, r = len(tiles(v)), rows(2 * v)
                nc.scalar.copy(v_hi[0:r, 2 * v:2 * v + w].rearrange("p a n -> p (a n)"),
                               ps[0:r, V_BANK[v], 0:256 * w]).then_inc(v_hi_done, 1)

            def exponentials(b, h, p, parts=(0, 1)):
                act.wait_ge(max_done, b * 8 + (4 * h + p + 1))
                for n in parts:
                    s0, s1 = ((0, 1024), (1024, S))[n]
                    nc.scalar.activation(prob[:, p, s0:s1], sc[:, s0:s1], ACT.Exp, bias=nmax[:, p:p + 1],
                                         accum_out=psums[:, p, n:n + 1]).then_inc(exp_done, 1)

            def turned(b, h, g, t):
                n = 7 * g + t
                act.wait_ge(pT_full, b * 28 + (14 * h + n + 1))
                w, r = 256 * len(tiles(t)), rows(2 * t)
                nc.scalar.copy(pT_hi[0:r, n % 2, 0:w], ps[0:r, 6 + n % 2, 0:w]).then_inc(pT_hi_done, 1)

            def sums(b, h, g):
                act.wait_ge(pv_full, b * 4 + (2 * h + g + 1))
                nc.scalar.copy(rsb[:, g], ps[:, 4 + g, 256:512]).then_inc(rsb_done, 1)

            def unit(b, h, last):
                nb, nh = (b, 1) if h == 0 else (b + 1, 0)

                def next_keys(g, t):
                    if not last and (g, t) in KEYS_AT:
                        keys(nb, nh, KEYS_AT[g, t])

                values(b, h, 0)
                exponentials(b, h, 0)
                values(b, h, 1)
                values(b, h, 2)
                exponentials(b, h, 1)
                for v in range(3, 6):
                    values(b, h, v)
                exponentials(b, h, 2)
                for v in range(6, NV):
                    values(b, h, v)
                for t in range(NV):
                    turned(b, h, 0, t)
                    if t in (1, 2):
                        exponentials(b, h, 3, (t - 1,))
                    next_keys(0, t)
                turned(b, h, 1, 0)
                next_keys(1, 0)
                sums(b, h, 0)
                for t in range(1, NV):
                    turned(b, h, 1, t)
                    next_keys(1, t)
                sums(b, h, 1)

            for n in range(8):
                keys(0, 0, n)
            with act.Fori(0, B - 1) as b:
                unit(b, 0, False)
                unit(b, 1, False)
            unit(B - 1, 0, False)
            unit(B - 1, 1, True)

        @block.vector
        def _(dve):
            def keys(b, h, n):
                c, m = n // 2, n % 2
                cols = slice(CW * c, CW * c + CW)
                dve.wait_ge(k_hi_done, b * 16 + (8 * h + n + 1))
                nc.vector.scalar_tensor_tensor(kT_lo[:, m, cols], ps[:, n % 4, 0:CW], bk[:, 2 * h + m:2 * h + m + 1],
                                               f32(kT_hi[:, m, cols]), ALU.add, ALU.subtract).then_inc(k_lo_done, 1)

            def values(b, h, v):
                w, r = len(tiles(v)), rows(2 * v)
                dve.wait_ge(v_hi_done, b * 14 + (7 * h + v + 1))
                nc.vector.tensor_tensor(v_lo[0:r, 2 * v:2 * v + w].rearrange("p a n -> p (a n)"),
                                        ps[0:r, V_BANK[v], 0:256 * w],
                                        f32(v_hi[0:r, 2 * v:2 * v + w].rearrange("p a n -> p (a n)")),
                                        ALU.subtract).then_inc(v_lo_done, 1)

            def maxima(b, h, p):
                for n, (s0, _, w) in enumerate(SC_CHUNKS):
                    dve.wait_ge(sc_full, b * 32 + (16 * h + 4 * p + n + 1))
                    nc.vector.tensor_reduce(pmax[:, p % 2, n:n + 1], ps[:, n, 0:w], AX.X, ALU.max).then_inc(pmax_done, 1)
                dve.wait_ge(pmax_done, b * 32 + (16 * h + 4 * p + 4))
                nc.vector.tensor_reduce(nmax[:, p:p + 1], pmax[:, p % 2], AX.X, ALU.max, negate=True).then_inc(max_done, 1)

            def sums(b, h, g):
                dve.wait_ge(exp_done, b * 16 + (8 * h + 4 * g + 4))
                nc.vector.tensor_tensor(rsum[:, g], psums[:, 2 * g:2 * g + 2, 0], psums[:, 2 * g:2 * g + 2, 1],
                                        ALU.add).then_inc(sum_step, 1)
                dve.wait_ge(sum_step, b * 8 + (4 * h + 2 * g + 1))
                nc.vector.reciprocal(rinv[:, g], rsum[:, g]).then_inc(sum_step, 1)
                dve.wait_ge(sum_step, b * 8 + (4 * h + 2 * g + 2))
                for j in range(2):
                    nc.vector.tensor_scalar(diag[:, g, j], ident[:], rinv[:, g, j:j + 1], None, ALU.mult).then_inc(diag_done, 1)

            def turned(b, h, g, t):
                n = 7 * g + t
                w, r = 256 * len(tiles(t)), rows(2 * t)
                dve.wait_ge(pT_hi_done, b * 28 + (14 * h + n + 1))
                nc.vector.tensor_tensor(pT_lo[0:r, n % 2, 0:w], ps[0:r, 6 + n % 2, 0:w], f32(pT_hi[0:r, n % 2, 0:w]),
                                        ALU.subtract).then_inc(pT_lo_done, 1)

            def output(b, h, g):
                dve.wait_ge(rsb_done, b * 4 + (2 * h + g + 1))
                for i in range(4):
                    q = slice(32 * i, 32 * i + 32)
                    c = slice(64 * i, 64 * i + 64)
                    ins = nc.vector.tensor_tensor(oT[q, 2 * h + g, bass.ds(b * L, L)], ps[q, 4 + g, c], rsb[q, g, c], ALU.mult)
                ins.then_inc(o_done, 1)

            def unit(b, h, last):
                nb, nh = (b, 1) if h == 0 else (b + 1, 0)

                def next_keys(g, t):
                    if not last and (g, t) in KEYS_AT:
                        keys(nb, nh, KEYS_AT[g, t])

                values(b, h, 0)
                maxima(b, h, 0)
                values(b, h, 1)
                values(b, h, 2)
                maxima(b, h, 1)
                values(b, h, 3)
                values(b, h, 4)
                maxima(b, h, 2)
                for v in range(5, NV):
                    values(b, h, v)
                sums(b, h, 0)
                turned(b, h, 0, 0)
                maxima(b, h, 3)
                for t in range(1, NV):
                    turned(b, h, 0, t)
                    next_keys(0, t)
                    if t == 4:
                        sums(b, h, 1)
                turned(b, h, 1, 0)
                next_keys(1, 0)
                output(b, h, 0)
                for t in range(1, NV):
                    turned(b, h, 1, t)
                    next_keys(1, t)
                output(b, h, 1)

            dve.sem_inc(o_done, 1)
            for n in range(8):
                keys(0, 0, n)
            with dve.Fori(0, B - 1) as b:
                unit(b, 0, False)
                unit(b, 1, False)
            unit(B - 1, 0, False)
            unit(B - 1, 1, True)


def normaliser(nc, sb, sem, name):
    stats, mv = sb(name + "_stats", [P, TT, 6]), sb(name + "_mv", [P, TT, 2])
    veps, std, rstd = (sb(f"{name}_{n}", [P, TT]) for n in ("veps", "std", "rstd"))
    step, std_done = sem(name + "_step"), sem(name + "_std_done")

    def on_vector(dve, src, dst, done, ready=None):
        for t in range(TT):
            if ready is not None:
                dve.wait_ge(ready, t + 1)
            ins = nc.vector.bn_stats(stats[:, t], src[:, t])
        ins.then_inc(step, 1)
        dve.wait_ge(step, 1)
        for t in range(TT):
            ins = nc.vector.bn_aggr(mv[:, t], stats[:, t])
        ins.then_inc(step, 1)
        dve.wait_ge(step, 2)
        nc.vector.tensor_scalar(veps[:], mv[:, :, 1], EPS, None, ALU.add).then_inc(step, 1)
        dve.wait_ge(std_done, 1)
        nc.vector.reciprocal(rstd[:], std[:]).then_inc(step, 1)
        dve.wait_ge(step, 4)
        for t in range(TT):
            nc.vector.tensor_scalar(dst[:, t], src[:, t], mv[:, t, 0:1], rstd[:, t:t + 1], ALU.subtract,
                                    ALU.mult).then_inc(done, 1)

    def on_scalar(act):
        act.wait_ge(step, 3)
        nc.scalar.activation(std[:], veps[:], ACT.Sqrt).then_inc(std_done, 1)

    return on_vector, on_scalar


def head_attention(nc, a, keep):
    ident, tokA, tokB = keep["ident"], keep["oT"], keep["x"]
    NR, NS, NP, NPV = 2, 3, 3, 2
    QR = 4
    NQ, NA = 2 * H2 // QR, H2 // QR
    PW = QR * 2 * H2 * D2
    with ExitStack() as ctx:
        def sb(name, shape, dt=F32):
            return ctx.enter_context(nc.sbuf_tensor(name, shape, dt))

        def sem(name):
            return ctx.enter_context(nc.semaphore(name))

        raw = sb("h_raw", [P, NR, KD, D])
        w_hi = [sb(f"h_w_hi{i}", [P, KD, D], F32R) for i in range(NS)]
        w_lo = [sb(f"h_w_lo{i}", [P, KD, D], F32R) for i in range(NS)]
        row = sb("h_row", [P, 2, D])
        cols = sb("h_cols", [P, 2, KD])
        lam4 = sb("h_lam4", [P, 4, D2])
        lprod, lsum, lexp = sb("h_lprod", [P, 2, D2]), sb("h_lsum", [P, 2]), sb("h_lexp", [P, 2])
        ldif, lam = sb("h_ldif", [P, 1]), sb("h_lam", [P, 1])
        a_hi, a_lo = sb("h_a_hi", [P, KD, T], F32R), sb("h_a_lo", [P, KD, T], F32R)
        hT = sb("h_hT", [P, KD, T])
        q = sb("h_q", [P, TT, 2 * H2, D2])
        k = sb("h_k", [P, TT, 2 * H2, D2])
        v = sb("h_v", [P, TT, 2 * D2, H2])
        prod, vprod = sb("h_prod", [P, NP, PW]), sb("h_vprod", [P, NPV, PW])
        att = sb("h_att", [P, 2, 2 * H2, 2 * H2])
        z1, z2 = sb("h_z1", [P, 4 * H2 * H2]), sb("h_z2", [P, 4 * H2 * H2])
        ex = sb("h_ex", [P, 2 * H2, 2 * H2])
        rmax, nmax, rsum = (sb(f"h_{n}", [P, 2 * H2]) for n in ("rmax", "nmax", "rsum"))
        rinv, rlam = sb("h_rinv", [P, 2 * H2]), sb("h_rlam", [P, H2])
        w0, w1, att2 = (sb(f"h_{n}", [P, H2, H2]) for n in ("w0", "w1", "att2"))
        o = sb("h_o", [P, 2, H2, 2 * D2])
        sq = sb("h_sq", [P, H2, 2 * D2])
        ms, mse, rms, rrms = (sb(f"h_{n}", [P, H2]) for n in ("ms", "mse", "rms", "rrms"))
        on = sb("h_on", [P, 2, D])
        ps = ctx.enter_context(nc.psum_tensor("ps_h", [P, 8, 512], F32))

        w_loaded = [sem(f"h_w_loaded{i}") for i in range(NR)]
        x_loaded, c_loaded = sem("h_x_loaded"), sem("h_c_loaded")
        whi_done, wlo_done = sem("h_whi_done"), sem("h_wlo_done")
        o_hi_done, o_lo_done = sem("h_o_hi_done"), sem("h_o_lo_done")
        xb_done, x1_full, x1_done = sem("h_xb_done"), sem("h_x1_full"), sem("h_x1_done")
        y_done, yn_done, yb_done = sem("h_y_done"), sem("h_yn_done"), sem("h_yb_done")
        tr_full, hT_done, h_hi_done, h_lo_done = (sem(f"h_{n}") for n in ("tr_full", "hT_done", "h_hi_done", "h_lo_done"))
        qkv_full, qkv_done = sem("h_qkv_full"), sem("h_qkv_done")
        lam_step, lexp_done = sem("h_lam_step"), sem("h_lexp_done")
        prod_done, vprod_done, red_done = sem("h_prod_done"), sem("h_vprod_done"), sem("h_red_done")
        z_done, zsum_done = sem("h_z_done"), sem("h_zsum_done")
        rmax_step, exp_done = sem("h_rmax_step"), sem("h_exp_done")
        rsum_step, w01_done, att2_done = sem("h_rsum_step"), sem("h_w01_done"), sem("h_att2_done")
        sq_done, ms_step, rms_done, on_done = sem("h_sq_done"), sem("h_ms_step"), sem("h_rms_done"), sem("h_on_done")
        aT_full, aT_hi_done, aT_lo_done = sem("h_aT_full"), sem("h_aT_hi_done"), sem("h_aT_lo_done")
        src_full, conn_done = sem("h_src_full"), sem("h_conn_done")
        norm1, norm1_act = normaliser(nc, sb, sem, "h_n1")
        norm2, norm2_act = normaliser(nc, sb, sem, "h_n2")

        block = ctx.enter_context(nc.Block())

        order, at_qk, at_av = [], {}, {}
        for t in range(TT + 1):
            for i in range(NQ if t < TT else 0):
                at_qk[t, i] = len(order)
                order.append(("qk", t, i))
            for i in range(NA if t else 0):
                at_av[t - 1, i] = len(order)
                order.append(("av", t - 1, i))

        by_vector = [n for n in range(len(order)) if n % 3 == 2]
        by_pool = [n for n in range(len(order)) if n % 3 != 2]

        def multiply(eng, n, buffer):
            kind, t, i = order[n]
            r = slice(QR * i, QR * i + QR)
            if kind == "qk":
                shape = [P, QR, 2 * H2, D2]
                return eng.tensor_tensor(buffer.rearrange("p (a b d) -> p a b d", a=QR, b=2 * H2),
                                         q[:, t, r].unsqueeze(2).to_broadcast(shape),
                                         k[:, t].unsqueeze(1).to_broadcast(shape), ALU.mult)
            shape = [P, QR, 2 * D2, H2]
            return eng.tensor_tensor(buffer.rearrange("p (a d h) -> p a d h", a=QR, d=2 * D2),
                                     att2[:, r].unsqueeze(2).to_broadcast(shape),
                                     v[:, t].unsqueeze(1).to_broadcast(shape), ALU.mult)

        @block.sync
        def _(sp):
            def load(s):
                if s >= NR:
                    sp.wait_ge(wlo_done, s - NR + 1)
                sp.dma_start(raw[:, s % NR], a["slabs"][s]).then_inc(w_loaded[s % NR], 16)
            load(0)
            sp.dma_start(tokB[:], a["x"].rearrange("(t p) d -> p t d", p=P)).then_inc(x_loaded, 16)
            sp.dma_start(row[:], a["rows"][0:2].partition_broadcast(P)).then_inc(x_loaded, 16)
            load(1)
            sp.dma_start(cols[:], a["ln1"]).then_inc(c_loaded, 16)
            sp.dma_start(lam4[:], a["lambdas"].partition_broadcast(P)).then_inc(c_loaded, 16)
            for s in range(2, 5):
                load(s)

        @block.gpsimd
        def _(pool):
            def low(s):
                pool.wait_ge(whi_done, s + 1)
                if s == 4:
                    pool.wait_ge(wlo_done, 4)
                nc.gpsimd.tensor_tensor(w_lo[s % NS][:], raw[:, s % NR], f32(w_hi[s % NS][:]), ALU.subtract).then_inc(wlo_done, 1)

            def product(n):
                if n not in by_pool:
                    return
                kind, t, _ = order[n]
                m = by_pool.index(n)
                if m >= NP:
                    pool.wait_ge(red_done, by_pool[m - NP] + 1)
                if kind == "qk":
                    pool.wait_ge(qkv_done, 3 * t + 2)
                else:
                    pool.wait_ge(att2_done, t + 1)
                multiply(nc.gpsimd, n, prod[:, m % NP]).then_inc(prod_done, 1)

            def add_z(t):
                pool.wait_ge(z_done, 2 * t + 2)
                nc.gpsimd.tensor_tensor(att[:, t % 2].rearrange("p a b -> p (a b)"), z1[:], z2[:], ALU.add).then_inc(zsum_done, 1)

            def weights(t):
                pool.wait_ge(rsum_step, 2 * t + 2)
                if t:
                    pool.wait_ge(att2_done, t)
                nc.gpsimd.tensor_tensor(w0[:], ex[:, 0:H2, 0:H2], rinv[:, 0:H2].unsqueeze(2).to_broadcast([P, H2, H2]),
                                        ALU.mult).then_inc(w01_done, 1)
                nc.gpsimd.tensor_tensor(w1[:], ex[:, H2:, H2:], rlam[:].unsqueeze(2).to_broadcast([P, H2, H2]),
                                        ALU.mult).then_inc(w01_done, 1)
                pool.wait_ge(w01_done, 2 * t + 2)
                if t:
                    pool.wait_ge(red_done, at_av[t - 1, NA - 1] + 1)
                nc.gpsimd.tensor_tensor(att2[:], w0[:], w1[:], ALU.subtract).then_inc(att2_done, 1)

            def square(t):
                pool.wait_ge(red_done, at_av[t, NA - 1] + 1)
                if t:
                    pool.wait_ge(ms_step, 3 * t)
                nc.gpsimd.tensor_tensor(sq[:], o[:, t % 2], o[:, t % 2], ALU.mult).then_inc(sq_done, 1)

            def scale(t):
                pool.wait_ge(ms_step, 3 * t + 3)
                if t >= 2:
                    pool.wait_ge(aT_full, t - 1)
                nc.gpsimd.tensor_tensor(on[:, t % 2].rearrange("p (a d) -> p a d", a=H2), o[:, t % 2],
                                        rrms[:].unsqueeze(2).to_broadcast([P, H2, 2 * D2]), ALU.mult).then_inc(on_done, 1)

            low(0)
            pool.wait_ge(x_loaded, 32)
            nc.gpsimd.tensor_tensor(tokB[:], tokB[:], row[:, 0].unsqueeze(1).to_broadcast([P, TT, D]), ALU.add).then_inc(xb_done, 1)
            for s in range(1, 4):
                low(s)
            pool.wait_ge(yn_done, TT)
            nc.gpsimd.tensor_tensor(tokA[:], tokA[:], row[:, 1].unsqueeze(1).to_broadcast([P, TT, D]), ALU.add).then_inc(yb_done, 1)
            for t in range(TT + 1):
                for i in range(NQ if t < TT else 0):
                    product(at_qk[t, i])
                    if t >= 2 and i == 1:
                        square(t - 2)
                    if t >= 2 and i == NQ - 1:
                        scale(t - 2)
                if t == TT:
                    square(t - 2)
                if t:
                    weights(t - 1)
                    product(at_av[t - 1, 0])
                if t < TT:
                    add_z(t)
                for i in range(1, NA if t else 0):
                    product(at_av[t - 1, i])
                if t == 1:
                    low(4)
                if t == TT:
                    scale(t - 2)
                    square(t - 1)
                    scale(t - 1)

        @block.scalar
        def _(act):
            def high(s):
                act.wait_ge(w_loaded[s % NR], 16 * (s // NR + 1))
                if s == 3:
                    act.wait_ge(x1_full, TT)
                if s == 4:
                    act.wait_ge(qkv_full, 3 * TT)
                nc.scalar.copy(w_hi[s % NS][:], raw[:, s % NR]).then_inc(whi_done, 1)

            for g in range(KD):
                nc.scalar.activation(a_hi[:, g], tokA[:, g], ACT.Identity, bias=keep["bv"][:, g:g + 1]).then_inc(o_hi_done, 1)
            for s in range(3):
                high(s)
            norm1_act(act)
            high(3)
            norm2_act(act)
            act.wait_ge(c_loaded, 32)
            act.wait_ge(tr_full, KD)
            for g in range(KD):
                nc.scalar.activation(hT[:, g], ps[:, 4 + g], ACT.Identity, bias=cols[:, 1, g:g + 1],
                                     scale=cols[:, 0, g:g + 1]).then_inc(hT_done, 1)
            act.wait_ge(lam_step, 2)
            nc.scalar.activation(lexp[:], lsum[:], ACT.Exp).then_inc(lexp_done, 1)
            for n in range(3 * TT):
                t, w = n // 3, n % 3
                act.wait_ge(qkv_full, n + 1)
                if w < 2:
                    nc.scalar.mul((q, k)[w][:, t].rearrange("p (c h) d -> p h d c", c=2),
                                  ps[:, n % 8].rearrange("p (h d c) -> p h d c", h=H2, c=2),
                                  (float(D2) ** -0.5, 1.0)[w]).then_inc(qkv_done, 1)
                else:
                    nc.scalar.copy(v[:, t].rearrange("p d h -> p h d"),
                                   ps[:, n % 8].rearrange("p (h d) -> p h d", h=H2)).then_inc(qkv_done, 1)
            high(4)
            def exponentials(t):
                act.wait_ge(rmax_step, 2 * t + 2)
                if t:
                    act.wait_ge(w01_done, 2 * t)
                for r in range(2 * H2):
                    ins = nc.scalar.activation(ex[:, r], att[:, t % 2, r], ACT.Exp, bias=nmax[:, r:r + 1],
                                               accum_out=rsum[:, r:r + 1])
                ins.then_inc(exp_done, 1)

            def normalised(t):
                act.wait_ge(ms_step, 3 * t + 2)
                nc.scalar.activation(rms[:], mse[:], ACT.Sqrt).then_inc(rms_done, 1)
                act.wait_ge(aT_full, t + 1)
                nc.scalar.copy(a_hi[:, :, P * t:P * t + P], ps[:, t].rearrange("p (k n) -> p k n", k=KD)).then_inc(aT_hi_done, 1)

            for t in range(TT):
                if t >= 2:
                    normalised(t - 2)
                exponentials(t)
            normalised(TT - 2)
            normalised(TT - 1)

        @block.vector
        def _(dve):
            def reduce(n):
                kind, t, i = order[n]
                r = slice(QR * i, QR * i + QR)
                out = att[:, t % 2, r] if kind == "qk" else o[:, t % 2, r]
                if kind == "av" and i == 0 and t >= 2:
                    dve.wait_ge(on_done, t - 1)
                if n in by_pool:
                    m = by_pool.index(n)
                    summed = prod[:, m % NP]
                    dve.wait_ge(prod_done, m + 1)
                else:
                    m = by_vector.index(n)
                    summed = vprod[:, m % NPV]
                    if m >= NPV:
                        dve.wait_ge(red_done, by_vector[m - NPV] + 1)
                    dve.wait_ge(*((qkv_done, 3 * t + 2) if kind == "qk" else (att2_done, t + 1)))
                    multiply(nc.vector, n, summed).then_inc(vprod_done, 1)
                    dve.wait_ge(vprod_done, m + 1)
                nc.vector.tensor_reduce(out, summed.rearrange("p (a b d) -> p a b d", a=QR, d=D2), AX.X,
                                        ALU.add).then_inc(red_done, 1)

            def clean(t):
                x = att[:, t % 2].rearrange("p a b -> p (a b)")
                dve.wait_ge(red_done, at_qk[t, NQ - 1] + 1)
                nc.vector.tensor_scalar(z1[:], x, 0.0, -FMAX, ALU.min, ALU.max).then_inc(z_done, 1)
                nc.vector.tensor_scalar(z2[:], x, 0.0, FMAX, ALU.max, ALU.min).then_inc(z_done, 1)

            def row_max(t):
                dve.wait_ge(zsum_done, t + 1)
                nc.vector.tensor_reduce(rmax[:], att[:, t % 2], AX.X, ALU.max).then_inc(rmax_step, 1)
                dve.wait_ge(rmax_step, 2 * t + 1)
                nc.vector.tensor_scalar(nmax[:], rmax[:], -1.0, None, ALU.mult).then_inc(rmax_step, 1)

            def row_sum(t):
                dve.wait_ge(exp_done, t + 1)
                nc.vector.reciprocal(rinv[:], rsum[:]).then_inc(rsum_step, 1)
                dve.wait_ge(rsum_step, 2 * t + 1)
                nc.vector.tensor_scalar(rlam[:], rinv[:, H2:], lam[:], None, ALU.mult).then_inc(rsum_step, 1)

            def mean_square(t):
                dve.wait_ge(sq_done, t + 1)
                nc.vector.tensor_reduce(ms[:], sq[:], AX.X, ALU.add).then_inc(ms_step, 1)
                dve.wait_ge(ms_step, 3 * t + 1)
                c = (1.0 - LAMBDA_INIT) ** -2
                nc.vector.tensor_scalar(mse[:], ms[:], c / (2 * D2), c * EPS, ALU.mult, ALU.add).then_inc(ms_step, 1)

            def root(t):
                dve.wait_ge(rms_done, t + 1)
                nc.vector.reciprocal(rrms[:], rms[:]).then_inc(ms_step, 1)

            def attended_low(t):
                dve.wait_ge(aT_hi_done, t + 1)
                s = slice(P * t, P * t + P)
                nc.vector.tensor_tensor(a_lo[:, :, s], ps[:, t].rearrange("p (k n) -> p k n", k=KD), f32(a_hi[:, :, s]),
                                        ALU.subtract).then_inc(aT_lo_done, 1)

            def skip(t):
                dve.wait_ge(src_full, t + 1)
                nc.vector.tensor_tensor(tokA[:, t], ps[:, 4 + t], tokA[:, t], ALU.add).then_inc(conn_done, 1)

            for g in range(KD):
                dve.wait_ge(o_hi_done, g + 1)
                nc.vector.scalar_tensor_tensor(a_lo[:, g], tokA[:, g], keep["bv"][:, g:g + 1], f32(a_hi[:, g]), ALU.add,
                                               ALU.subtract).then_inc(o_lo_done, 1)
            dve.wait_ge(c_loaded, 32)
            nc.vector.tensor_tensor(lprod[:], lam4[:, 0:2], lam4[:, 2:4], ALU.mult).then_inc(lam_step, 1)
            dve.wait_ge(lam_step, 1)
            nc.vector.tensor_reduce(lsum[:], lprod[:], AX.X, ALU.add).then_inc(lam_step, 1)
            dve.wait_ge(xb_done, 1)
            for t in range(TT):
                dve.wait_ge(x1_full, t + 1)
                nc.vector.tensor_tensor(tokB[:, t], ps[:, t], tokB[:, t], ALU.add).then_inc(x1_done, 1)
            norm1(dve, tokB, tokA, y_done, x1_done)
            norm2(dve, tokA, hT, yn_done, y_done)
            for g in range(KD):
                dve.wait_ge(hT_done, g + 1)
                nc.vector.tensor_copy(a_hi[:, g], hT[:, g]).then_inc(h_hi_done, 1)
                dve.wait_ge(h_hi_done, g + 1)
                nc.vector.tensor_tensor(a_lo[:, g], hT[:, g], f32(a_hi[:, g]), ALU.subtract).then_inc(h_lo_done, 1)
            dve.wait_ge(lexp_done, 1)
            nc.vector.tensor_tensor(ldif[:], lexp[:, 0:1], lexp[:, 1:2], ALU.subtract).then_inc(lam_step, 1)
            dve.wait_ge(lam_step, 3)
            nc.vector.tensor_scalar(lam[:], ldif[:], LAMBDA_INIT, None, ALU.add).then_inc(lam_step, 1)
            dve.wait_ge(lam_step, 4)
            dve.wait_ge(yb_done, 1)
            for t in range(TT + 1):
                for i in range(NQ if t < TT else 0):
                    reduce(at_qk[t, i])
                    if t >= 2 and i == 2:
                        mean_square(t - 2)
                    if t and i == 4:
                        row_sum(t - 1)
                    if t >= 2 and i == 5:
                        root(t - 2)
                    if t >= 2 and i == 7:
                        attended_low(t - 2)
                if t == TT:
                    row_sum(t - 1)
                    mean_square(t - 2)
                    root(t - 2)
                if t < TT:
                    clean(t)
                for i in range(2 if t else 0):
                    reduce(at_av[t - 1, i])
                if t < TT:
                    row_max(t)
                for i in range(2, NA if t else 0):
                    reduce(at_av[t - 1, i])
                if t == TT:
                    attended_low(t - 2)
                if t >= 2:
                    skip(t - 2)
            mean_square(TT - 1)
            root(TT - 1)
            attended_low(TT - 1)
            skip(TT - 1)

        @block.tensor
        def _(pe):
            pe.wait_ge(wlo_done, 1)
            for t in range(TT):
                for g in range(KD):
                    if t == 0:
                        pe.wait_ge(o_lo_done, g + 1)
                    ins = mm3(nc, ps[:, t], a_hi[:, g, P * t:P * t + P], a_lo[:, g, P * t:P * t + P], w_hi[0][:, g], w_lo[0][:, g],
                              g == 0, g == KD - 1)
                ins.then_inc(x1_full, 1)
            for g in range(KD):
                for t in range(TT):
                    if g == 0:
                        pe.wait_ge(yn_done, t + 1)
                    ins = nc.tensor.transpose(ps[:, 4 + g, P * t:P * t + P], hT[:, t, P * g:P * g + P], ident[:])
                ins.then_inc(tr_full, 1)
            pe.wait_ge(h_lo_done, KD)
            pe.wait_ge(x1_done, TT)
            for n in range(3 * TT):
                t, w = n // 3, n % 3
                s = 1 + w
                if t == 0:
                    pe.wait_ge(wlo_done, s + 1)
                if n >= 8:
                    pe.wait_ge(qkv_done, n - 7)
                for g in range(KD):
                    ins = mm3(nc, ps[:, n % 8], a_hi[:, g, P * t:P * t + P], a_lo[:, g, P * t:P * t + P], w_hi[s % NS][:, g],
                              w_lo[s % NS][:, g], g == 0, g == KD - 1)
                ins.then_inc(qkv_full, 1)
            pe.wait_ge(qkv_done, 3 * TT)
            pe.wait_ge(wlo_done, 5)
            for t in range(TT):
                pe.wait_ge(on_done, t + 1)
                for g in range(KD):
                    ins = nc.tensor.transpose(ps[:, t, P * g:P * g + P], on[:, t % 2, P * g:P * g + P], ident[:])
                ins.then_inc(aT_full, 1)
                pe.wait_ge(aT_lo_done, t + 1)
                for g in range(KD):
                    ins = mm3(nc, ps[:, 4 + t], a_hi[:, g, P * t:P * t + P], a_lo[:, g, P * t:P * t + P], w_hi[4 % NS][:, g],
                              w_lo[4 % NS][:, g], g == 0, g == KD - 1)
                ins.then_inc(src_full, 1)


def feed_forward(nc, a, keep):
    ident, tokA, tokB = keep["ident"], keep["oT"], keep["x"]
    NR, NS, NF, NSLAB, FT = 3, 5, 3, 8, FF // P
    with ExitStack() as ctx:
        def sb(name, shape, dt=F32):
            return ctx.enter_context(nc.sbuf_tensor(name, shape, dt))

        def sem(name):
            return ctx.enter_context(nc.semaphore(name))

        raw = sb("f_raw", [P, NR, KD, D])
        w_hi = [sb(f"f_w_hi{i}", [P, KD, D], F32R) for i in range(NS)]
        w_lo = [sb(f"f_w_lo{i}", [P, KD, D], F32R) for i in range(NS)]
        row = sb("f_row", [P, D])
        cols = sb("f_cols", [P, 2, KD])
        b1 = sb("f_b1", [P, FT])
        a_hi, a_lo = sb("f_a_hi", [P, KD, T], F32R), sb("f_a_lo", [P, KD, T], F32R)
        cn = sb("f_cn", [P, TT, D])
        hT = sb("f_hT", [P, KD, T])
        fT = sb("f_fT", [P, NF, T])
        f_hi, f_lo = sb("f_f_hi", [P, NF, T], F32R), sb("f_f_lo", [P, NF, T], F32R)
        ps = ctx.enter_context(nc.psum_tensor("ps_f", [P, 8, 512], F32))

        w_loaded = [sem(f"f_w_loaded{i}") for i in range(NR)]
        c_loaded, b_loaded = sem("f_c_loaded"), sem("f_b_loaded")
        whi_done, wlo_done = sem("f_whi_done"), sem("f_wlo_done")
        cn_done, skip_done = sem("f_cn_done"), sem("f_skip_done")
        tr_full, hT_done, h_hi_done, h_lo_done = (sem(f"f_{n}") for n in ("tr_full", "hT_done", "h_hi_done", "h_lo_done"))
        up_full, f_done, f_hi_done, f_lo_done = (sem(f"f_{n}") for n in ("up_full", "f_done", "f_hi_done", "f_lo_done"))
        down_full, x2_done = sem("f_down_full"), sem("f_x2_done")
        norm, norm_act = normaliser(nc, sb, sem, "f_n")

        block = ctx.enter_context(nc.Block())
        behind = {5: 4, 6: 6, 7: 8}

        @block.sync
        def _(sp):
            for s in range(NSLAB):
                if s >= NR:
                    sp.wait_ge(wlo_done, s - NR + 1)
                sp.dma_start(raw[:, s % NR], a["slabs"][5 + s]).then_inc(w_loaded[s % NR], 16)
                if s == 0:
                    sp.dma_start(cols[:], a["ln2"]).then_inc(c_loaded, 16)
                    sp.dma_start(b1[:], a["b1"]).then_inc(c_loaded, 16)
                    sp.dma_start(row[:], a["rows"][2].partition_broadcast(P)).then_inc(b_loaded, 16)

        @block.gpsimd
        def _(pool):
            def low(s):
                pool.wait_ge(whi_done, s + 1)
                nc.gpsimd.tensor_tensor(w_lo[s % NS][:], raw[:, s % NR], f32(w_hi[s % NS][:]), ALU.subtract).then_inc(wlo_done, 1)

            for s in range(NS):
                low(s)
            pool.wait_ge(b_loaded, 16)
            pool.wait_ge(cn_done, TT)
            nc.gpsimd.tensor_tensor(tokA[:], tokA[:], row[:].unsqueeze(1).to_broadcast([P, TT, D]), ALU.add).then_inc(skip_done, 1)
            pool.wait_ge(skip_done, 1)
            nc.gpsimd.tensor_tensor(tokB[:], tokA[:], tokB[:], ALU.add).then_inc(skip_done, 1)
            for f in range(FT):
                pool.wait_ge(f_hi_done, f + 1)
                nc.gpsimd.tensor_tensor(f_lo[:, f % NF], fT[:, f % NF], f32(f_hi[:, f % NF]), ALU.subtract).then_inc(f_lo_done, 1)
                for s in [s for s, after in behind.items() if after == f]:
                    low(s)

        @block.scalar
        def _(act):
            def high(s):
                act.wait_ge(w_loaded[s % NR], 16 * (s // NR + 1))
                if s >= NS:
                    used = s - NS
                    act.wait_ge(down_full if used % 2 else up_full, 4 * (used // 2) + 4)
                nc.scalar.copy(w_hi[s % NS][:], raw[:, s % NR]).then_inc(whi_done, 1)

            high(0)
            norm_act(act)
            high(1)
            act.wait_ge(c_loaded, 32)
            for g in range(KD):
                act.wait_ge(tr_full, g + 1)
                nc.scalar.activation(hT[:, g], ps[:, g], ACT.Identity, bias=cols[:, 1, g:g + 1],
                                     scale=cols[:, 0, g:g + 1]).then_inc(hT_done, 1)
            for s in range(2, NS):
                high(s)
            for f in range(FT):
                act.wait_ge(up_full, f + 1)
                if f >= NF:
                    act.wait_ge(f_lo_done, f - NF + 1)
                nc.scalar.activation(fT[:, f % NF], ps[:, 4 + f % 4], ACT.Relu, bias=b1[:, f:f + 1]).then_inc(f_done, 1)
                for s in [s for s, after in behind.items() if after == f]:
                    high(s)

        @block.vector
        def _(dve):
            norm(dve, tokA, cn, cn_done)
            for g in range(KD):
                dve.wait_ge(hT_done, g + 1)
                nc.vector.tensor_copy(a_hi[:, g], hT[:, g]).then_inc(h_hi_done, 1)
                dve.wait_ge(h_hi_done, g + 1)
                nc.vector.tensor_tensor(a_lo[:, g], hT[:, g], f32(a_hi[:, g]), ALU.subtract).then_inc(h_lo_done, 1)
            for f in range(FT):
                dve.wait_ge(f_done, f + 1)
                if f >= NF:
                    dve.wait_ge(down_full, f - NF + 1)
                nc.vector.tensor_copy(f_hi[:, f % NF], fT[:, f % NF]).then_inc(f_hi_done, 1)
            dve.wait_ge(skip_done, 2)
            dve.wait_ge(down_full, FT)
            for t in range(TT):
                nc.vector.tensor_tensor(tokB[:, t], ps[:, t], tokB[:, t], ALU.add).then_inc(x2_done, 1)

        @block.tensor
        def _(pe):
            for g in range(KD):
                for t in range(TT):
                    if g == 0:
                        pe.wait_ge(cn_done, t + 1)
                    ins = nc.tensor.transpose(ps[:, g, P * t:P * t + P], cn[:, t, P * g:P * g + P], ident[:])
                ins.then_inc(tr_full, 1)
            pe.wait_ge(h_lo_done, KD)

            def up(f):
                s = 2 * (f // 4)
                if f % 4 == 0:
                    pe.wait_ge(wlo_done, s + 1)
                if f >= 4:
                    pe.wait_ge(f_done, f - 3)
                c = slice(P * (f % 4), P * (f % 4) + P)
                for g in range(KD):
                    ins = mm3(nc, ps[:, 4 + f % 4], w_hi[s % NS][:, g, c], w_lo[s % NS][:, g, c], a_hi[:, g], a_lo[:, g],
                              g == 0, g == KD - 1)
                ins.then_inc(up_full, 1)

            def down(f):
                s = 2 * (f // 4) + 1
                if f % 4 == 0:
                    pe.wait_ge(wlo_done, s + 1)
                pe.wait_ge(f_lo_done, f + 1)
                for t in range(TT):
                    c = slice(P * t, P * t + P)
                    ins = mm3(nc, ps[:, t], f_hi[:, f % NF, c], f_lo[:, f % NF, c], w_hi[s % NS][:, f % 4], w_lo[s % NS][:, f % 4],
                              f == 0, f == FT - 1)
                ins.then_inc(down_full, 1)

            for f in range(FT + 2):
                if f < FT:
                    up(f)
                if f >= 2:
                    down(f - 2)


def route(nc, a, keep):
    ident, ones, x2 = keep["ident"], keep["ones"], keep["x"]
    WG, WE = KD * 2 * I, KD * 2 * I + (I // P) * D
    with ExitStack() as ctx:
        def sb(name, shape, dt=F32):
            return ctx.enter_context(nc.sbuf_tensor(name, shape, dt))

        def sem(name):
            return ctx.enter_context(nc.semaphore(name))

        xm = sb("r_xm", [P, TT, D])
        m_hi, m_lo = sb("r_m_hi", [P, KD, T], F32R), sb("r_m_lo", [P, KD, T], F32R)
        gate = sb("r_gate", [P, 2, KD, E])
        g_hi, g_lo = sb("r_g_hi", [P, KD, E], F32R), sb("r_g_lo", [P, KD, E], F32R)
        bias = sb("r_bias", [P, E])
        before = sb("r_before", [P, P])
        score, sfc = sb("r_score", [P, TT, E]), sb("r_sfc", [P, TT, E])
        gmax, gtop = sb("r_gmax", [P, TT, NG]), sb("r_gtop", [P, TT, 8])
        ggt, geq, gcum, gsel = (sb(f"r_{n}", [P, TT, NG]) for n in ("ggt", "geq", "gcum", "gsel"))
        gleft = sb("r_gleft", [P, TT])
        masked, etop = sb("r_masked", [P, TT, E]), sb("r_etop", [P, TT, 8])
        egt, eeq, ecum, esel = (sb(f"r_{n}", [P, TT, E]) for n in ("egt", "eeq", "ecum", "esel"))
        eleft = sb("r_eleft", [P, TT])
        weight, wsum, winv = sb("r_weight", [P, TT, E]), sb("r_wsum", [P, TT]), sb("r_winv", [P, TT])
        onesE = sb("r_ones", [P, E])
        nblk, cblk, base = sb("r_nblk", [P, E]), sb("r_cblk", [P, E]), sb("r_base", [P, E])
        pos = sb("r_pos", [P, TT, E])
        ends = sb("r_ends", [P, NBLK, E])
        owner, owner_f = sb("r_owner", [P, NBLK]), sb("r_owner_f", [P, NBLK])
        turns = sb("r_turns", [P, NBLK // U])
        nturn = sb("r_nturn", [P, 1])
        raw = sb("r_raw", [P, 2, WE])
        w_hi, w_lo = sb("r_w_hi", [P, 2, WE], F32R), sb("r_w_lo", [P, 2, WE], F32R)
        sg, t1, hid = sb("r_sg", [P, 2, T]), sb("r_t1", [P, 2, T]), sb("r_hid", [P, 2, T])
        h_hi, h_lo = sb("r_h_hi", [P, 2, 2, T], F32R), sb("r_h_lo", [P, 2, 2, T], F32R)
        ps = ctx.enter_context(nc.psum_tensor("ps_r", [P, 8, 512], F32))

        g_loaded, b_loaded, xm_stored = sem("r_g_loaded"), sem("r_b_loaded"), sem("r_xm_stored")
        w_loaded = [sem(f"r_w_loaded{i}") for i in range(2)]
        ghi_done, glo_done = sem("r_ghi_done"), sem("r_glo_done")
        xm_done, tr_full, m_hi_done, m_lo_done = sem("r_xm_done"), sem("r_tr_full"), sem("r_m_hi_done"), sem("r_m_lo_done")
        logit_full, score_done = sem("r_logit_full"), sem("r_score_done")
        step, sel_done, rank_full = sem("r_step"), sem("r_sel_done"), sem("r_rank_full")
        whi_done, wlo_done = sem("r_whi_done"), sem("r_wlo_done")
        up_full, sg_done, t1_done, hid_done, h_hi_done, h_lo_done, down_full = (
            sem(f"r_{n}") for n in ("up_full", "sg_done", "t1_done", "hid_done", "h_hi_done", "h_lo_done", "down_full"))
        norm, norm_act = normaliser(nc, sb, sem, "r_n")

        block = ctx.enter_context(nc.Block())

        def gu(w, s):
            return w[:, s, 0:WG].rearrange("p (k n) -> p k n", k=KD)

        def dn(w, s):
            return w[:, s, WG:WE].rearrange("p (k n) -> p k n", k=I // P)

        @block.sync
        def _(sp):
            sp.dma_start(gate[:, 0], a["gateT"]).then_inc(g_loaded, 16)
            sp.dma_start(bias[:], a["e_bias"].partition_broadcast(P)).then_inc(b_loaded, 16)
            sp.dma_start(before[:], a["before"]).then_inc(b_loaded, 16)
            sp.dma_start(keep["slot"][:], a["slot"].partition_broadcast(P)).then_inc(b_loaded, 16)
            sp.dma_start(keep["token"][:], a["token"]).then_inc(b_loaded, 16)
            for s in range(2):
                sp.dma_start(raw[:, s], a["shared"][s]).then_inc(w_loaded[s], 16)
            sp.wait_ge(xm_done, TT)
            sp.dma_start(a["xm_dram"].rearrange("(t p) d -> p t d", p=P), xm[:]).then_inc(xm_stored, 16)
            sp.wait_ge(xm_stored, 16)

        @block.gpsimd
        def _(pool):
            pool.wait_ge(ghi_done, 1)
            nc.gpsimd.tensor_tensor(g_lo[:], gate[:, 0], f32(g_hi[:]), ALU.subtract).then_inc(glo_done, 1)
            for s in range(2):
                pool.wait_ge(whi_done, s + 1)
                nc.gpsimd.tensor_tensor(w_lo[:, s], raw[:, s], f32(w_hi[:, s]), ALU.subtract).then_inc(wlo_done, 1)
            for n in range(4):
                s, m = n // 2, n % 2
                pool.wait_ge(h_hi_done, n + 1)
                nc.gpsimd.tensor_tensor(h_lo[:, s, m], hid[:, m], f32(h_hi[:, s, m]), ALU.subtract).then_inc(h_lo_done, 1)

        @block.scalar
        def _(act):
            act.wait_ge(g_loaded, 16)
            nc.scalar.copy(g_hi[:], gate[:, 0]).then_inc(ghi_done, 1)
            act.wait_ge(w_loaded[0], 16)
            nc.scalar.copy(w_hi[:, 0], raw[:, 0]).then_inc(whi_done, 1)
            norm_act(act)
            for g in range(KD):
                act.wait_ge(tr_full, g + 1)
                nc.scalar.copy(m_hi[:, g], ps[:, g]).then_inc(m_hi_done, 1)
            act.wait_ge(logit_full, 1)
            nc.scalar.activation(score[:].rearrange("p t e -> p (t e)"), ps[:, 0, 0:TT * E], ACT.Sigmoid).then_inc(score_done, 1)
            act.wait_ge(w_loaded[1], 16)
            nc.scalar.copy(w_hi[:, 1], raw[:, 1]).then_inc(whi_done, 1)
            for n in range(4):
                act.wait_ge(up_full, n + 1)
                if n >= 2:
                    act.wait_ge(t1_done, n - 1)
                nc.scalar.activation(sg[:, n % 2], ps[:, 4 + 2 * (n % 2)], ACT.Sigmoid).then_inc(sg_done, 1)

        @block.vector
        def _(dve):
            steps = [0]

            def link(ins):
                steps[0] += 1
                ins.then_inc(step, 1)
                dve.wait_ge(step, steps[0])

            def first(n, values, top, gt, eq, cum, left, sel, width):
                for t in range(TT):
                    ins = nc.vector.max(top[:, t], values[:, t])
                link(ins)
                level = top[:, :, n - 1:n].to_broadcast([P, TT, width])
                nc.vector.tensor_tensor(gt[:], values[:], level, ALU.is_gt)
                link(nc.vector.tensor_tensor(eq[:], values[:], level, ALU.is_equal))
                for t in range(TT):
                    nc.vector.tensor_tensor_scan(cum[:, t], onesE[:, 0:width], eq[:, t], 0.0, ALU.mult, ALU.add)
                link(nc.vector.tensor_reduce(left[:], gt[:], AX.X, ALU.add))
                link(nc.vector.tensor_scalar(left[:], left[:], -1.0, float(n), ALU.mult, ALU.add))
                link(nc.vector.tensor_tensor(cum[:], cum[:], left[:].unsqueeze(2).to_broadcast([P, TT, width]), ALU.is_le))
                link(nc.vector.tensor_tensor(eq[:], eq[:], cum[:], ALU.mult))
                link(nc.vector.tensor_tensor(sel[:], gt[:], eq[:], ALU.add))

            def hidden(s):
                for m in range(2):
                    n = 2 * s + m
                    dve.wait_ge(sg_done, n + 1)
                    if n >= 2:
                        dve.wait_ge(h_lo_done, n - 1)
                    nc.vector.tensor_tensor(t1[:, m], ps[:, 4 + 2 * m], sg[:, m], ALU.mult).then_inc(t1_done, 1)
                    dve.wait_ge(t1_done, n + 1)
                    nc.vector.tensor_tensor(hid[:, m], ps[:, 5 + 2 * m], t1[:, m], ALU.mult).then_inc(hid_done, 1)
                    dve.wait_ge(hid_done, n + 1)
                    nc.vector.tensor_copy(h_hi[:, s, m], hid[:, m]).then_inc(h_hi_done, 1)

            nc.vector.memset(onesE[:], 1.0)
            norm(dve, x2, xm, xm_done)
            for g in range(KD):
                dve.wait_ge(m_hi_done, g + 1)
                nc.vector.tensor_tensor(m_lo[:, g], ps[:, g], f32(m_hi[:, g]), ALU.subtract).then_inc(m_lo_done, 1)
            dve.wait_ge(b_loaded, 64)
            dve.wait_ge(score_done, 1)
            link(nc.vector.tensor_tensor(sfc[:], score[:], bias[:].unsqueeze(1).to_broadcast([P, TT, E]), ALU.add))
            link(nc.vector.tensor_reduce(gmax[:], sfc[:].rearrange("p t (g s) -> p t g s", g=NG), AX.X, ALU.max))
            first(TOPKG, gmax, gtop, ggt, geq, gcum, gleft, gsel, NG)
            for t in range(TT):
                ins = nc.vector.tensor_tensor(masked[:, t].rearrange("p (g s) -> p g s", g=NG),
                                              sfc[:, t].rearrange("p (g s) -> p g s", g=NG),
                                              gsel[:, t].unsqueeze(2).to_broadcast([P, NG, GS]), ALU.mult)
            link(ins)
            first(TOPK, masked, etop, egt, eeq, ecum, eleft, esel, E)
            nc.vector.tensor_tensor(weight[:], score[:], esel[:], ALU.mult).then_inc(sel_done, 1)
            dve.wait_ge(sel_done, 1)
            link(nc.vector.tensor_reduce(wsum[:], weight[:], AX.X, ALU.add))
            link(nc.vector.tensor_scalar(wsum[:], wsum[:], 1e-20, None, ALU.add))
            link(nc.vector.reciprocal(winv[:], wsum[:]))
            link(nc.vector.tensor_scalar(winv[:], winv[:], SCALE, None, ALU.mult))
            facts = keep["fact"][:].rearrange("p e (t f) -> p t e f", t=TT)
            token = keep["token"][:].unsqueeze(2).to_broadcast([P, TT, E])
            nc.vector.tensor_copy(facts[:, :, :, 0], token)
            nc.vector.tensor_copy(facts[:, :, :, 2], onesE[:].unsqueeze(1).to_broadcast([P, TT, E]))
            nc.vector.tensor_copy(facts[:, :, :, 5], onesE[:].unsqueeze(1).to_broadcast([P, TT, E]))
            for t in range(TT):
                nc.vector.tensor_tensor_scan(ecum[:, t], onesE[:], esel[:, t], 0.0, ALU.mult, ALU.add)
            link(nc.vector.tensor_tensor(weight[:], weight[:], winv[:].unsqueeze(2).to_broadcast([P, TT, E]), ALU.mult))
            link(nc.vector.tensor_copy(facts[:, :, :, 3], weight[:]))
            nc.vector.tensor_tensor(facts[:, :, :, 4], weight[:], f32(facts[:, :, :, 3]), ALU.subtract)
            link(nc.vector.scalar_tensor_tensor(facts[:, :, :, 1], token, float(TOPK), ecum[:], ALU.mult, ALU.add))
            count = ps[:, 1, 0:E]
            dve.wait_ge(rank_full, 1)
            link(nc.vector.tensor_scalar(nblk[:], count, 0.0, None, ALU.is_gt))
            for m in range(1, TT):
                link(nc.vector.scalar_tensor_tensor(nblk[:], count, float(P * m), nblk[:], ALU.is_gt, ALU.add))
            link(nc.vector.tensor_tensor_scan(cblk[:], onesE[:], nblk[:], 0.0, ALU.mult, ALU.add))
            link(nc.vector.tensor_tensor(base[:], cblk[:], nblk[:], ALU.subtract))
            link(nc.vector.scalar_tensor_tensor(pos[:], base[:].unsqueeze(1).to_broadcast([P, TT, E]), float(P),
                                                ps[:, 1, E:E * (TT + 1)].rearrange("p (t e) -> p t e", t=TT), ALU.mult, ALU.add))
            link(nc.vector.scalar_tensor_tensor(pos[:], pos[:], 1.0, esel[:], ALU.add, ALU.mult))
            link(nc.vector.tensor_scalar(keep["place"][:].rearrange("p e t -> p t e"), pos[:], -1.0, None, ALU.add))
            j_row = keep["slot"][:, P:P + NBLK]
            link(nc.vector.tensor_tensor(ends[:], cblk[:].unsqueeze(1).to_broadcast([P, NBLK, E]),
                                         j_row.unsqueeze(2).to_broadcast([P, NBLK, E]), ALU.is_le))
            link(nc.vector.tensor_reduce(owner[:], ends[:], AX.X, ALU.add))
            link(nc.vector.tensor_scalar(owner_f[:], owner[:], float(E - 1), None, ALU.min))
            link(nc.vector.tensor_copy(keep["owner"][:], owner_f[:]))
            link(nc.vector.tensor_scalar(turns[:], keep["slot"][:, P:P + NBLK:U], cblk[:, E - 1:E], None, ALU.is_lt))
            link(nc.vector.tensor_reduce(nturn[:], turns[:], AX.X, ALU.add))
            link(nc.vector.tensor_copy(keep["nturn"][:], nturn[:]))
            hidden(0)
            hidden(1)
            dve.wait_ge(down_full, 2)
            for t in range(TT):
                nc.vector.tensor_tensor(x2[:, t], ps[:, t], x2[:, t], ALU.add)

        @block.tensor
        def _(pe):
            def up(s):
                pe.wait_ge(wlo_done, s + 1)
                for m in range(2):
                    if s:
                        pe.wait_ge(hid_done, m + 1)
                    for u in range(2):
                        c = slice(I * u + P * m, I * u + P * m + P)
                        for g in range(KD):
                            ins = mm3(nc, ps[:, 4 + 2 * m + u], gu(w_hi, s)[:, g, c], gu(w_lo, s)[:, g, c], m_hi[:, g], m_lo[:, g],
                                      g == 0, g == KD - 1)
                    ins.then_inc(up_full, 1)

            def down(s):
                for m in range(2):
                    pe.wait_ge(h_lo_done, 2 * s + m + 1)
                    for t in range(TT):
                        c = slice(P * t, P * t + P)
                        ins = mm3(nc, ps[:, t], h_hi[:, s, m, c], h_lo[:, s, m, c], dn(w_hi, s)[:, m], dn(w_lo, s)[:, m],
                                  s == 0 and m == 0, s == 1 and m == 1)
                ins.then_inc(down_full, 1)

            for g in range(KD):
                for t in range(TT):
                    if g == 0:
                        pe.wait_ge(xm_done, t + 1)
                    ins = nc.tensor.transpose(ps[:, g, P * t:P * t + P], xm[:, t, P * g:P * g + P], ident[:])
                ins.then_inc(tr_full, 1)
            pe.wait_ge(glo_done, 1)
            pe.wait_ge(m_lo_done, KD)
            for t in range(TT):
                c = slice(P * t, P * t + P)
                for g in range(KD):
                    ins = mm3(nc, ps[:, 0, E * t:E * t + E], m_hi[:, g, c], m_lo[:, g, c], g_hi[:, g], g_lo[:, g],
                              g == 0, g == KD - 1)
            ins.then_inc(logit_full, 1)
            up(0)
            pe.wait_ge(b_loaded, 64)
            pe.wait_ge(sel_done, 1)
            for t in range(TT):
                nc.tensor.matmul(ps[:, 1, 0:E], ones[:], esel[:, t], start=(t == 0), stop=(t == TT - 1))
            for t in range(TT):
                c = slice(E * (t + 1), E * (t + 2))
                for u in range(t):
                    nc.tensor.matmul(ps[:, 1, c], ones[:], esel[:, u], start=(u == 0), stop=False)
                ins = nc.tensor.matmul(ps[:, 1, c], before[:], esel[:, t], start=(t == 0), stop=True)
            ins.then_inc(rank_full, 1)
            up(1)
            down(0)
            down(1)


def experts(nc, a, keep):
    ident, x2 = keep["ident"], keep["x"]
    place, fact, slot = keep["place"], keep["fact"], keep["slot"]
    AHEAD = 3
    FAR = float(1 << 20)
    PAIRS = T * TOPK
    with ExitStack() as ctx:
        def sb(name, shape, dt=F32):
            return ctx.enter_context(nc.sbuf_tensor(name, shape, dt))

        def sem(name):
            return ctx.enter_context(nc.semaphore(name))

        w_gu = sb("e_w_gu", [P, U, KD, 2 * I])
        w_dn = sb("e_w_dn", [P, U, I // P, D])
        one = sb("e_one", [P, 1])
        rel = sb("e_rel", [P, U, TT])
        pick = sb("e_pick", [P, U, TT, P], F32R)
        facts = sb("e_facts", [P, U, TT, NF], F32R)
        info = sb("e_info", [P, U, NF])
        share = sb("e_share", [P, U])
        row_in = sb("e_row_in", [P, U], mybir.dt.uint32)
        far = sb("e_far", [P, U])
        row_out = sb("e_row_out", [P, U], mybir.dt.uint32)
        xg = sb("e_xg", [P, U, D])
        xT = sb("e_xT", [P, U, D])
        sg, t1, hid = (sb(f"e_{n}", [P, U, I]) for n in ("sg", "t1", "hid"))
        hT = sb("e_hT", [P, U, I])
        y = sb("e_y", [P, U, D])
        six = sb("e_six", [P, 2, TOPK, D])
        total, out = sb("e_total", [P, TT, D]), sb("e_out", [P, TT, D])
        ps = ctx.enter_context(nc.psum_tensor("ps_e", [P, 8, 512], F32))
        INFO, XT, GU, HT, DN = range(5)

        gu_loaded = [sem(f"e_gu_loaded{i}") for i in range(U)]
        dn_loaded = [sem(f"e_dn_loaded{i}") for i in range(U)]
        gathered = [sem(f"e_gathered{i}") for i in range(U)]
        scattered = [sem(f"e_scattered{i}") for i in range(U)]
        rel_done, facts_done, pick_done = sem("e_rel_done"), sem("e_facts_done"), sem("e_pick_done")
        info_full, info_done, row_in_done = sem("e_info_full"), sem("e_info_done"), sem("e_row_in_done")
        far_done, row_out_done, share_done = sem("e_far_done"), sem("e_row_out_done"), sem("e_share_done")
        xT_full, xT_done = sem("e_xT_full"), sem("e_xT_done")
        gu_full, sg_done, t1_done, hid_done = sem("e_gu_full"), sem("e_sg_done"), sem("e_t1_done"), sem("e_hid_done")
        hT_full, hT_done, dn_full, y_done = sem("e_hT_full"), sem("e_hT_done"), sem("e_dn_full"), sem("e_y_done")
        six_loaded = [sem(f"e_six_loaded{i}") for i in range(2)]
        started = sem("e_started")
        total_done, out_done, stored = sem("e_total_done"), sem("e_out_done"), sem("e_stored")

        block = ctx.enter_context(nc.Block())

        def turns(eng):
            return eng.value_load(keep["nturn"][0:1, 0:1], min_val=T * TOPK // P // U, max_val=-(-MAXB // U))

        def owner(eng, j):
            return eng.value_load(keep["owner"][0:1, bass.ds(j, 1)], min_val=0, max_val=E - 1)

        def nth(i, r, per=1, plus=0):
            return i * (U * per) + (r * per + plus)

        def wait_turn(eng, signal, value):
            if not isinstance(value, int):
                value = eng.to_reg(value)
            eng.wait_ge(started, 1)
            eng.wait_ge(signal, value)

        def landed(i, r):
            return i * 16 + 16 * (r // U + 1)

        @block.sync
        def _(sp):
            def gate_up(i, r, first=False):
                e = owner(sp, nth(i, r))
                if not first:
                    wait_turn(sp, gu_full, nth(i, r, plus=1 - U))
                sp.dma_start(w_gu[:, r % U], a["w_gu"][e]).then_inc(gu_loaded[r % U], 16)

            def down(i, r, first=False):
                e = owner(sp, nth(i, r))
                if not first:
                    wait_turn(sp, dn_full, nth(i, r, plus=1 - U))
                sp.dma_start(w_dn[:, r % U], a["w_dn"][e]).then_inc(dn_loaded[r % U], 16)

            for r in range(U):
                gate_up(0, r, True)
                down(0, r, True)
            gate_up(0, U)
            n = turns(sp)
            with sp.Fori(0, n) as i:
                for r in range(U):
                    down(i, r + U)
                    gate_up(i, r + U + 1)
            for r in range(U):
                wait_turn(sp, scattered[r], n * 16)
            for t in range(TT):
                if t >= 2:
                    sp.wait_ge(total_done, t - 1)
                sp.dma_start(six[:, t % 2], a["y_dram"][PAIRS // TT * t:PAIRS // TT * (t + 1)]
                             .rearrange("(p j) d -> p j d", j=TOPK)).then_inc(six_loaded[t % 2], 16)
            for t in range(TT):
                sp.wait_ge(out_done, t + 1)
                sp.dma_start(a["out"][P * t:P * t + P], out[:, t]).then_inc(stored, 16)
            sp.wait_ge(stored, 16 * TT)

        @block.gpsimd
        def _(pool):
            def gather(i, r):
                wait_turn(pool, row_in_done, nth(i, r, plus=1))
                nc.gpsimd.indirect_dma_start(out=xg[:, r % U], out_offset=None, in_=a["xm_dram"],
                                             in_offset=bass.IndirectOffsetOnAxis(ap=row_in[:, r % U:r % U + 1], axis=0)
                                             ).then_inc(gathered[r % U], 16)

            def scatter(i, r):
                wait_turn(pool, row_out_done, nth(i, r, plus=1))
                wait_turn(pool, y_done, nth(i, r, plus=1))
                nc.gpsimd.indirect_dma_start(out=a["y_dram"], out_offset=bass.IndirectOffsetOnAxis(ap=row_out[:, r % U:r % U + 1], axis=0),
                                             in_=y[:, r % U], in_offset=None, bounds_check=PAIRS - 1, oob_is_err=False
                                             ).then_inc(scattered[r % U], 16)

            for r in range(AHEAD):
                gather(0, r)
            with pool.Fori(0, turns(pool)) as i:
                for r in range(U):
                    gather(i, r + AHEAD)
                    scatter(i, r)

        @block.vector
        def _(dve):
            nc.vector.memset(one[:], 1.0).then_inc(started, 1)

            def pick_slots(i, r):
                b = r % U
                j = nth(i, r)
                e = owner(dve, j)
                if not isinstance(i, int) or r >= U:
                    dve.wait_ge(info_full, nth(i, r, plus=1 - U))
                nc.vector.tensor_tensor(rel[:, b], place[:, bass.ds(e, 1)].squeeze(1),
                                        slot[:, bass.ds(j + (P + NBLK), 1)].to_broadcast([P, TT]), ALU.subtract).then_inc(rel_done, 1)
                nc.vector.tensor_copy(facts[:, b].rearrange("p t f -> p (t f)"), fact[:, bass.ds(e, 1)].squeeze(1)).then_inc(facts_done, 1)
                dve.wait_ge(rel_done, nth(i, r, plus=1))
                for t in range(TT):
                    ins = nc.vector.tensor_scalar(pick[:, b, t], slot[:, 0:P], rel[:, b, t:t + 1], None, ALU.is_equal)
                ins.then_inc(pick_done, 1)

            def rows_in(i, r):
                b = r % U
                dve.wait_ge(info_full, nth(i, r, plus=1))
                if not isinstance(i, int) or r >= U:
                    dve.wait_ge(gathered[b], landed(i, r - U))
                nc.vector.tensor_copy(info[:, b], ps[:, INFO, 0:NF]).then_inc(info_done, 1)
                dve.wait_ge(info_done, nth(i, r, plus=1))
                nc.vector.tensor_copy(row_in[:, b:b + 1], info[:, b, 0:1]).then_inc(row_in_done, 1)

            def hidden(i, r):
                b = r % U
                if not isinstance(i, int) or r >= U:
                    dve.wait_ge(scattered[b], landed(i, r - U))
                nc.vector.tensor_tensor(share[:, b:b + 1], info[:, b, 3:4], info[:, b, 4:5], ALU.add).then_inc(share_done, 1)
                nc.vector.tensor_scalar(far[:, b:b + 1], info[:, b, 2:3], -FAR, FAR - 1.0, ALU.mult, ALU.add).then_inc(far_done, 1)
                dve.wait_ge(far_done, nth(i, r, plus=1))
                nc.vector.tensor_tensor(row_out[:, b:b + 1], info[:, b, 1:2], far[:, b:b + 1], ALU.add).then_inc(row_out_done, 1)
                dve.wait_ge(sg_done, nth(i, r, plus=1))
                nc.vector.tensor_tensor(t1[:, b], ps[:, GU, 0:I], sg[:, b], ALU.mult).then_inc(t1_done, 1)
                dve.wait_ge(share_done, nth(i, r, plus=1))
                dve.wait_ge(t1_done, nth(i, r, plus=1))
                nc.vector.scalar_tensor_tensor(hid[:, b], ps[:, GU, I:2 * I], share[:, b:b + 1], t1[:, b], ALU.mult,
                                               ALU.mult).then_inc(hid_done, 1)

            for r in range(AHEAD):
                pick_slots(0, r)
                rows_in(0, r)
            hidden(0, 0)
            pick_slots(0, AHEAD)
            with dve.Fori(0, turns(dve)) as i:
                for r in range(U):
                    rows_in(i, r + AHEAD)
                    pick_slots(i, r + AHEAD + 1)
                    hidden(i, r + 1)
            for t in range(TT):
                dve.wait_ge(six_loaded[t % 2], 16 * (t // 2 + 1))
                nc.vector.tensor_reduce(total[:, t], six[:, t % 2].rearrange("p j d -> p d j"), AX.X, ALU.add).then_inc(total_done, 1)
                dve.wait_ge(total_done, t + 1)
                nc.vector.tensor_tensor(out[:, t], total[:, t], x2[:, t], ALU.add).then_inc(out_done, 1)

        @block.scalar
        def _(act):
            def turned(i, r):
                act.wait_ge(xT_full, nth(i, r, plus=1))
                nc.scalar.copy(xT[:, r % U], ps[:, XT]).then_inc(xT_done, 1)

            def gates(i, r):
                act.wait_ge(gu_full, nth(i, r, plus=1))
                nc.scalar.activation(sg[:, r % U], ps[:, GU, 0:I], ACT.Sigmoid).then_inc(sg_done, 1)

            def hidden_turned(i, r):
                act.wait_ge(hT_full, nth(i, r, plus=1))
                nc.scalar.copy(hT[:, r % U], ps[:, HT, 0:I]).then_inc(hT_done, 1)

            turned(0, 0)
            turned(0, 1)
            gates(0, 0)
            with act.Fori(0, turns(act)) as i:
                for r in range(U):
                    turned(i, r + 2)
                    hidden_turned(i, r)
                    gates(i, r + 1)
                    act.wait_ge(row_out_done, nth(i, r, plus=1))
                    act.wait_ge(dn_full, nth(i, r, plus=1))
                    nc.scalar.copy(y[:, r % U], ps[:, DN]).then_inc(y_done, 1)

        @block.tensor
        def _(pe):
            def look_up(i, r):
                b = r % U
                pe.wait_ge(pick_done, nth(i, r, plus=1))
                if not isinstance(i, int) or r:
                    pe.wait_ge(info_done, nth(i, r))
                for t in range(TT):
                    ins = nc.tensor.matmul(ps[:, INFO, 0:NF], pick[:, b, t], facts[:, b, t], start=(t == 0), stop=(t == TT - 1))
                ins.then_inc(info_full, 1)

            def turn(i, r):
                b = r % U
                pe.wait_ge(gathered[b], landed(i, r))
                if not isinstance(i, int) or r:
                    pe.wait_ge(xT_done, nth(i, r))
                for g in range(KD):
                    ins = nc.tensor.transpose(ps[:, XT, P * g:P * g + P], xg[:, b, P * g:P * g + P], ident[:])
                ins.then_inc(xT_full, 1)

            def gate_up(i, r):
                b = r % U
                pe.wait_ge(gu_loaded[b], landed(i, r))
                pe.wait_ge(xT_done, nth(i, r, plus=1))
                for g in range(KD):
                    ins = nc.tensor.matmul(ps[:, GU], xT[:, b, P * g:P * g + P], w_gu[:, b, g], start=(g == 0), stop=(g == KD - 1))
                ins.then_inc(gu_full, 1)

            def turn_hidden(i, r):
                b = r % U
                pe.wait_ge(hid_done, nth(i, r, plus=1))
                for m in range(I // P):
                    ins = nc.tensor.transpose(ps[:, HT, P * m:P * m + P], hid[:, b, P * m:P * m + P], ident[:])
                ins.then_inc(hT_full, 1)

            def down(i, r):
                b = r % U
                pe.wait_ge(dn_loaded[b], landed(i, r))
                pe.wait_ge(hT_done, nth(i, r, plus=1))
                for m in range(I // P):
                    ins = nc.tensor.matmul(ps[:, DN], hT[:, b, P * m:P * m + P], w_dn[:, b, m], start=(m == 0), stop=(m == I // P - 1))
                ins.then_inc(dn_full, 1)

            for r in range(AHEAD):
                look_up(0, r)
            turn(0, 0)
            turn(0, 1)
            gate_up(0, 0)
            n = turns(pe)
            with pe.Fori(0, n) as i:
                for r in range(U):
                    look_up(i, r + AHEAD)
                    turn(i, r + 2)
                    turn_hidden(i, r)
                    gate_up(i, r + 1)
                    down(i, r)
            for r in range(U):
                pe.wait_ge(dn_loaded[r], n * 16 + 16)
                pe.wait_ge(gu_loaded[r], n * 16 + (32 if r == 0 else 16))
                pe.wait_ge(gathered[r], n * 16 + 16)


INPUTS = ("x", "identity", "b_Q", "b_K", "b_V", "w_qkv", "ctxT", "slabs", "rows", "ln1", "ln2", "b1", "lambdas",
          "gateT", "e_bias", "before", "slot", "token", "shared", "w_gu", "w_dn")


def build(nc, a):
    a["qbd_dram"] = nc.dram_tensor("qbd_dram", (2 * B, P, 512), F32, kind="Internal").ap()
    a["xm_dram"] = nc.dram_tensor("xm_dram", (T, D), F32, kind="Internal").ap()
    a["y_dram"] = nc.dram_tensor("y_dram", (T * TOPK, D), F32, kind="Internal").ap()
    with ExitStack() as ctx:
        def sb(stack, name, shape, dt=F32):
            return stack.enter_context(nc.sbuf_tensor(name, shape, dt))

        keep = {"ident": sb(ctx, "ident", [P, P]), "ones": sb(ctx, "ones", [P, P]), "bk": sb(ctx, "bk", [P, KD]),
                "bv": sb(ctx, "bv", [P, KD]), "oT": sb(ctx, "oT", [P, KD, T])}
        with ExitStack() as own:
            keep["wkv_hi"] = sb(own, "wkv_hi", [P, KD, 2 * D], F32R)
            keep["wkv_lo"] = sb(own, "wkv_lo", [P, KD, 2 * D], F32R)
            queries(nc, a, keep)
            cross_attention(nc, a, keep)
        keep["x"] = sb(ctx, "x_tok", [P, TT, D])
        head_attention(nc, a, keep)
        feed_forward(nc, a, keep)
        keep["slot"] = sb(ctx, "slot_sb", [P, P + 2 * NBLK])
        keep["token"] = sb(ctx, "token_sb", [P, TT])
        keep["place"] = sb(ctx, "place", [P, E, TT])
        keep["fact"] = sb(ctx, "fact", [P, E, TT * NF], F32R)
        keep["owner"] = sb(ctx, "owner", [P, NBLK], mybir.dt.int32)
        keep["nturn"] = sb(ctx, "nturn", [P, 1], mybir.dt.int32)
        route(nc, a, keep)
        experts(nc, a, keep)


def _by_rows(w):
    return np.ascontiguousarray(w.reshape(-1, P, w.shape[1]).transpose(1, 0, 2))


def _by_column(v):
    return np.ascontiguousarray(v.reshape(-1, P).T)


def _layout(i):
    x, h, f = (lambda n: i["L0_xattn_" + n]), (lambda n: i["L0_attn_" + n]), (lambda n: i["L0_ffn_" + n])
    ctx = np.zeros((B, SP_, D), np.float32)
    ctx[:, :S] = i["ctx_1024"]
    slabs = [x("W_O"), h("Wq").T, h("Wk").T, h("Wv").T, h("Wo").T]
    for n in range(FF // D):
        slabs += [h("W1").T[:, D * n:D * n + D], h("W2").T[D * n:D * n + D]]
    gu, dn = f("experts_gate_up").transpose(0, 2, 1), f("experts_down").transpose(0, 2, 1)
    sg, su, sd = f("shared_gate_w").T, f("shared_up_w").T, f("shared_down_w").T
    shared = []
    for n in range(2):
        s = slice(I * n, I * n + I)
        shared.append(np.concatenate([_by_rows(np.concatenate([sg[:, s], su[:, s]], 1)).reshape(P, -1),
                                      _by_rows(sd[s]).reshape(P, -1)], 1))
    blocks = np.arange(NBLK, dtype=np.float32)
    return {
        "x": i["x"].reshape(T, D),
        "identity": np.eye(P, dtype=np.float32),
        "b_Q": _by_column(x("b_Q")), "b_K": _by_column(x("b_K")), "b_V": _by_column(x("b_V")),
        "w_qkv": np.stack([_by_rows(x("W_" + n)) for n in "QKV"]),
        "ctxT": np.ascontiguousarray(ctx.reshape(B, NCH, CW, KD, P).transpose(0, 1, 4, 3, 2)).reshape(B * NCH, P, KD, CW),
        "slabs": np.stack([_by_rows(w) for w in slabs]),
        "rows": np.stack([x("b_O"), h("bo"), h("b2")]),
        "ln1": np.stack([_by_column(h("ln1_g")), _by_column(h("ln1_b"))], 1),
        "ln2": np.stack([_by_column(h("ln2_g")), _by_column(h("ln2_b"))], 1),
        "b1": _by_column(h("b1")),
        "lambdas": np.stack([h("lq1"), h("lq2"), h("lk1"), h("lk2")]),
        "gateT": _by_rows(f("gate_weight").T),
        "e_bias": f("e_score_correction_bias"),
        "before": np.triu(np.ones((P, P), np.float32), 1),
        "slot": np.concatenate([np.arange(P, dtype=np.float32), blocks, P * blocks]),
        "token": _by_column(np.arange(T, dtype=np.float32)),
        "shared": np.stack(shared),
        "w_gu": np.stack([_by_rows(w) for w in gu]),
        "w_dn": np.stack([_by_rows(w) for w in dn]),
    }


def kernel(**inputs):
    import concourse.bacc as bacc
    from concourse.bass_utils import run_bass_kernel_spmd

    arrays = _layout({n: np.asarray(v) for n, v in inputs.items()})
    nc = bacc.Bacc("TRN2", target_bir_lowering=False, num_devices=1)
    args = {n: nc.dram_tensor(n, arrays[n].shape, F32, kind="ExternalInput").ap() for n in INPUTS}
    args["out"] = nc.dram_tensor("out", (T, D), F32, kind="ExternalOutput").ap()
    build(nc, args)
    result = run_bass_kernel_spmd(nc, [{n: np.ascontiguousarray(v) for n, v in arrays.items()}], core_ids=[0])
    return result.results[0]["out"].reshape(B, L, D)
```
